# Optimizing a Trainium2 kernel written in Bass

```python
import numpy as np
import jax
import jax.numpy as jnp

def _softmax(x, axis=-1):
    return jax.nn.softmax(x, axis=axis)

def _gelu(x):
    return jax.nn.gelu(x, approximate=True)

def _silu(x):
    return jax.nn.silu(x)

def _sigmoid(x):
    return jax.nn.sigmoid(x)

def _layernorm(x, axis=-1, eps=1e-05):
    m = jnp.mean(x, axis=axis, keepdims=True)
    v = jnp.var(x, axis=axis, keepdims=True)
    return (x - m) / jnp.sqrt(v + eps)

def _scatter_add(tgt, idx, src, axis=0):
    return tgt.at[idx].add(src)

def _segment_sum(src, seg, n):
    return jax.ops.segment_sum(src, seg, n)
kernel_name = 'mk_sandwich_d1_jaxref_r8_afa8ab'

def setup_inputs(seed: int=0):
    np.random.seed(seed)
    _w = jnp.asarray

    def _L0_attn_setup():
        import jax, jax.numpy as jnp
        import numpy as np
        import math
        CTX_LEN = 96
        N_EMBD = 128

        def _depthwise_causal_conv(z, w, T, C):
            return jax.lax.conv_general_dilated(z, w, window_strides=(1,), padding=[(T - 1, 0)], feature_group_count=C, dimension_numbers=('NCH', 'OIH', 'NCH'))
        key = jax.random.key(seed)
        ks = jax.random.split(key, 8)
        B, T, C = (8, CTX_LEN, N_EMBD)
        x = jax.random.normal(ks[0], (B, T, C), dtype=jnp.float32)
        time_decay = jax.random.normal(ks[1], (C, 1), dtype=jnp.float32) * 0.1
        time_first = jnp.full((C, 1), math.log(0.3), dtype=jnp.float32)
        time_mix = jax.random.uniform(ks[2], (1, 1, C), dtype=jnp.float32)
        s = 0.02
        Wk = jax.random.normal(ks[3], (C, C), dtype=jnp.float32) * s
        Wv = jax.random.normal(ks[4], (C, C), dtype=jnp.float32) * s
        Wr = jax.random.normal(ks[5], (C, C), dtype=jnp.float32) * s
        Wo = jax.random.normal(ks[6], (C, C), dtype=jnp.float32) * s
        return {'x': x, 'time_decay': time_decay, 'time_first': time_first, 'time_mix': time_mix, 'Wk': Wk, 'Wv': Wv, 'Wr': Wr, 'Wo': Wo}
    _L0_attn_in = _L0_attn_setup()

    def _L0_ffn_setup():
        import jax, jax.numpy as jnp
        import numpy as np
        D = 128
        E = 8
        H = 256
        TOP_K = 2
        ALPHA = 0.5
        LN_EPS = 1e-05

        def _experts_all(x, W1, b1, W2, b2):
            h = jax.nn.relu(jnp.einsum('bld,edh->eblh', x, W1) + b1[:, None, None, :])
            return jnp.einsum('eblh,ehd->ebld', h, W2) + b2[:, None, None, :]

        def _selected_expert(x, expert_idx, W1, b1, W2, b2):
            oh = jax.nn.one_hot(expert_idx, E, dtype=x.dtype)
            return jnp.einsum('ebld,ble->bld', _experts_all(x, W1, b1, W2, b2), oh)

        def _layer_norm(x, gamma, beta):
            mu = jnp.mean(x, axis=-1, keepdims=True)
            var = jnp.mean(jnp.square(x - mu), axis=-1, keepdims=True)
            return (x - mu) * jax.lax.rsqrt(var + LN_EPS) * gamma + beta
        key = jax.random.key(seed)
        ks = jax.random.split(key, 8)
        x = jax.random.normal(ks[0], (2, 256, D), dtype=jnp.float32)
        gate_W = jax.random.normal(ks[1], (D, E), dtype=jnp.float32) * 0.02
        gate_b = jnp.zeros((E,), dtype=jnp.float32)
        W1 = jax.random.normal(ks[2], (E, D, H), dtype=jnp.float32) * 0.02
        b1 = jnp.zeros((E, H), dtype=jnp.float32)
        W2 = jax.random.normal(ks[3], (E, H, D), dtype=jnp.float32) * 0.02
        b2 = jnp.zeros((E, D), dtype=jnp.float32)
        ln_gamma = jnp.ones((D,), dtype=jnp.float32)
        ln_beta = jnp.zeros((D,), dtype=jnp.float32)
        return {'x': x, 'gate_W': gate_W, 'gate_b': gate_b, 'W1': W1, 'b1': b1, 'W2': W2, 'b2': b2, 'ln_gamma': ln_gamma, 'ln_beta': ln_beta}
    _L0_ffn_in = _L0_ffn_setup()
    _d = {'L0_attn_x': _L0_attn_in['x'], 'L0_attn_time_decay': _L0_attn_in['time_decay'], 'L0_attn_time_first': _L0_attn_in['time_first'], 'L0_attn_time_mix': _L0_attn_in['time_mix'], 'L0_attn_Wk': _L0_attn_in['Wk'], 'L0_attn_Wv': _L0_attn_in['Wv'], 'L0_attn_Wr': _L0_attn_in['Wr'], 'L0_attn_Wo': _L0_attn_in['Wo'], 'L0_ffn_gate_W': _L0_ffn_in['gate_W'], 'L0_ffn_gate_b': _L0_ffn_in['gate_b'], 'L0_ffn_W1': _L0_ffn_in['W1'], 'L0_ffn_b1': _L0_ffn_in['b1'], 'L0_ffn_W2': _L0_ffn_in['W2'], 'L0_ffn_b2': _L0_ffn_in['b2'], 'L0_ffn_ln_gamma': _L0_ffn_in['ln_gamma'], 'L0_ffn_ln_beta': _L0_ffn_in['ln_beta']}
    _x0 = _d['L0_attn_x']
    _d['L0_attn_x'] = jax.random.normal(jax.random.fold_in(jax.random.key(seed), 1), (2, 1024, 128), dtype=_x0.dtype)
    del _x0
    return _d

def reference(L0_attn_x, L0_attn_time_decay, L0_attn_time_first, L0_attn_time_mix, L0_attn_Wk, L0_attn_Wv, L0_attn_Wr, L0_attn_Wo, L0_ffn_gate_W, L0_ffn_gate_b, L0_ffn_W1, L0_ffn_b1, L0_ffn_W2, L0_ffn_b2, L0_ffn_ln_gamma, L0_ffn_ln_beta):

    def _L0_attn_ref(x, time_decay, time_first, time_mix, Wk, Wv, Wr, Wo):
        import jax, jax.numpy as jnp
        import numpy as np
        import math
        CTX_LEN = 96
        N_EMBD = 128

        def _depthwise_causal_conv(z, w, T, C):
            return jax.lax.conv_general_dilated(z, w, window_strides=(1,), padding=[(T - 1, 0)], feature_group_count=C, dimension_numbers=('NCH', 'OIH', 'NCH'))
        B, T, C = x.shape
        xs = jnp.pad(x, ((0, 0), (1, 0), (0, 0)))[:, :-1]
        xm = x * time_mix + xs * (1.0 - time_mix)
        k = jnp.einsum('btc,dc->bdt', xm, Wk)
        v = jnp.einsum('btc,dc->bdt', xm, Wv)
        r = jnp.einsum('btc,dc->btd', xm, Wr)
        k = jnp.exp(jnp.minimum(k, 60.0))
        kv = k * v
        time_curve = (jnp.arange(T - 1, dtype=jnp.float32) - (T - 2))[None, :]
        time_w = jnp.concatenate([jnp.exp(time_decay) * time_curve, time_first], axis=-1)
        w = jnp.exp(time_w)[:, None, :]
        wkv = _depthwise_causal_conv(kv, w, T, C)
        wk = _depthwise_causal_conv(k, w, T, C) + 1e-09
        rwkv = jax.nn.sigmoid(r) * jnp.swapaxes(wkv / wk, 1, 2)
        return jnp.einsum('btc,dc->btd', rwkv, Wo)

    def _L0_ffn_ref(x, gate_W, gate_b, W1, b1, W2, b2, ln_gamma, ln_beta):
        import jax, jax.numpy as jnp
        import numpy as np
        D = 128
        E = 8
        H = 256
        TOP_K = 2
        ALPHA = 0.5
        LN_EPS = 1e-05

        def _experts_all(x, W1, b1, W2, b2):
            h = jax.nn.relu(jnp.einsum('bld,edh->eblh', x, W1) + b1[:, None, None, :])
            return jnp.einsum('eblh,ehd->ebld', h, W2) + b2[:, None, None, :]

        def _selected_expert(x, expert_idx, W1, b1, W2, b2):
            oh = jax.nn.one_hot(expert_idx, E, dtype=x.dtype)
            return jnp.einsum('ebld,ble->bld', _experts_all(x, W1, b1, W2, b2), oh)

        def _layer_norm(x, gamma, beta):
            mu = jnp.mean(x, axis=-1, keepdims=True)
            var = jnp.mean(jnp.square(x - mu), axis=-1, keepdims=True)
            return (x - mu) * jax.lax.rsqrt(var + LN_EPS) * gamma + beta
        residual = x
        gate_logits = jnp.einsum('bld,de->ble', x, gate_W) + gate_b
        gate_weights = jax.nn.softmax(gate_logits, axis=-1)
        topk_vals, topk_idx = jax.lax.top_k(gate_weights, TOP_K)
        boost = jax.lax.stop_gradient(x)
        outs = []
        for i in range(TOP_K):
            eo = _selected_expert(boost, topk_idx[:, :, i], W1, b1, W2, b2)
            outs.append(eo)
            if i < TOP_K - 1:
                boost = boost + ALPHA * jax.lax.stop_gradient(eo)
        fused = sum((topk_vals[:, :, i:i + 1] * outs[i] for i in range(TOP_K)))
        return _layer_norm(residual + fused, ln_gamma, ln_beta)
    x = L0_attn_x
    x = x + _layernorm(_L0_attn_ref(_layernorm(x, axis=-1), L0_attn_time_decay, L0_attn_time_first, L0_attn_time_mix, L0_attn_Wk, L0_attn_Wv, L0_attn_Wr, L0_attn_Wo), axis=-1)
    x = x + _layernorm(_L0_ffn_ref(_layernorm(x, axis=-1), L0_ffn_gate_W, L0_ffn_gate_b, L0_ffn_W1, L0_ffn_b1, L0_ffn_W2, L0_ffn_b2, L0_ffn_ln_gamma, L0_ffn_ln_beta), axis=-1)
    return x

_drawn_inputs = setup_inputs


def setup_inputs(seed=0):
    import zlib

    import numpy as np

    out = dict(_drawn_inputs(seed))
    spreads = {'L0_attn_time_first': (-1.2039728164672852, 0.2),
     'L0_ffn_gate_b': (0.0, 0.8),
     'L0_ffn_b1': (0.0, 0.8),
     'L0_ffn_b2': (0.0, 0.8),
     'L0_ffn_ln_gamma': (1.0, 0.2),
     'L0_ffn_ln_beta': (0.0, 0.1)}
    factors = {'L0_ffn_gate_W': 6.116, 'L0_ffn_W1': 8.0, 'L0_ffn_W2': 8.0}
    for name, (base, spread) in spreads.items():
        noise = np.random.default_rng([zlib.crc32(name.encode()), seed]).standard_normal(out[name].shape)
        drawn = base * np.exp(spread * noise) if base else spread * noise
        out[name] = jnp.asarray(drawn.astype(out[name].dtype))
    for name, factor in factors.items():
        out[name] = (out[name] * factor).astype(out[name].dtype)
    return out
```

```python
from contextlib import ExitStack

import concourse.bass as bass
from concourse import mybir

ALU = mybir.AluOpType
ACT = mybir.ActivationFunctionType
AXX = mybir.AxisListType.X
F32 = mybir.dt.float32
BF16 = mybir.dt.bfloat16
I32 = mybir.dt.int32

P = 128
LN_EPS = 1e-5
K_MAX = 60.0
WK_EPS = 1e-9
ALPHA = 0.5
CHUNK = 512
TPC = CHUNK // P
AUX = 8
A_MEAN, A_RSTD, A_G0, A_G1, A_POS2, A_TOK = range(6)
BIG = 3.0e38


def build_program(nc, x, time_decay, time_first, time_mix, wk, wv, wr, wo,
                  gate_w, gate_b, w1, b1, w2, b2, ln_gamma, ln_beta, out):
    B, T, C = x.shape
    E, _, H = w1.shape
    TOKENS = B * T
    NT = TOKENS // P
    NQ = TOKENS // CHUNK
    QPB = T // CHUNK
    HC = H // P
    SLOT_TILES = NT + E - 1
    SLOTS = SLOT_TILES * P
    ROW1 = C + AUX
    ROW2 = 2 * C + ROW1
    FILL = 1 << 20
    assert C == P and T % CHUNK == 0 and H == HC * P

    xt_dram = x.rearrange("b t c -> (b t) c").rearrange("(n p) c -> p n c", p=P)
    out_rows = out.rearrange("b t c -> (b t) c")
    sorted1 = nc.dram_tensor("sorted1", (SLOTS, ROW1), F32, kind="Internal").ap()
    sorted2 = nc.dram_tensor("sorted2", (SLOTS, ROW2), F32, kind="Internal").ap()
    s1_tiles = sorted1.rearrange("(s p) w -> p s w", p=P)
    s2_tiles = sorted2.rearrange("(s p) w -> p s w", p=P)

    with ExitStack() as ctx:
        def sb(name, shape, dt=F32):
            return ctx.enter_context(nc.sbuf_tensor(name, shape, dt))

        def sem(name):
            return ctx.enter_context(nc.semaphore(name))

        bank = [ctx.enter_context(nc.psum_tensor(f"bank{i}", [P, 512], F32)) for i in range(8)]

        wnat = sb("wnat", [P, 4, C])
        wT = sb("wT", [P, 4, C])
        decay_in = sb("decay_in", [P, 1])
        first_in = sb("first_in", [P, 1])
        mix = sb("mix", [P, 1])
        mix_rest = sb("mix_rest", [P, 1])
        decay_e = sb("decay_e", [P, 1])
        decay = sb("decay", [P, 1])
        first = sb("first", [P, 1])
        wk_eps = sb("wk_eps", [P, 1])
        gw = sb("gw", [P, E])
        gb = sb("gb", [P, E])
        w1_all = sb("w1_all", [P, E, H + HC])
        b1_rows = sb("b1_rows", [E * HC, P])
        w2_all = sb("w2_all", [P, E * HC, C])
        b2_row = sb("b2_row", [1, E * C])
        gamma = sb("gamma", [P, C])
        beta = sb("beta", [P, C])
        ident = sb("ident", [P, P])
        before = sb("before", [P, P], BF16)
        ones_b = sb("ones_b", [P, P], BF16)
        ones_row = sb("ones_row", [1, P])
        minus_half = sb("minus_half", [P, NT])
        e_minus = sb("e_minus", [P, E, NT])
        tile_start = sb("tile_start", [P, 2, E, NT])
        slot_tile = sb("slot_tile", [1, 2, SLOT_TILES, E])
        tile_keep = sb("tile_keep", [P, 2, E, NT])
        keep_e = sb("keep_e", [P, 2, E])
        fill = sb("fill", [P, ROW2])

        rows3 = sb("rows3", [P, SLOT_TILES, ROW2])
        area = rows3[:].rearrange("p s w -> p (s w)")
        taken = [0]

        def over_rows3(*shape):
            size = shape[0] * shape[1]
            at = taken[0]
            taken[0] += size
            assert taken[0] <= SLOT_TILES * ROW2
            return area[:, at:at + size].rearrange("p (a b) -> p a b", b=shape[1])

        xin = sb("xin", [P, NT, C])
        st = sb("st", [P, 3, NT, 6])
        mv = sb("mv", [P, 3, NT, 2])
        veps = sb("veps", [P, 3, NT])
        rs = sb("rs", [P, 3, NT])
        xn = sb("xn", [P, NT, C])
        xnT = over_rows3(B, T + 1)
        xmix = over_rows3(2, CHUNK)
        xm = over_rows3(3, CHUNK)
        kc = over_rows3(2, CHUNK)
        ke = sb("ke", [P, 2, CHUNK])
        kv = over_rows3(2, CHUNK)
        th = over_rows3(2, CHUNK)
        sg = sb("sg", [P, 2, CHUNK])
        uk = sb("uk", [P, 2, CHUNK])
        sum_k = sb("sum_k", [P, B, T + 1])
        sum_kv = sb("sum_kv", [P, B, T + 1])
        wkv = sb("wkv", [P, 2, CHUNK])
        wks = sb("wks", [P, 2, CHUNK])
        rec = sb("rec", [P, 2, CHUNK])
        yq = sb("yq", [P, 2, CHUNK])
        rw = sb("rw", [P, 2, CHUNK])
        on = sb("on", [P, 2, TPC, C])
        rows1 = sb("rows1", [P, NT, ROW1])
        xn2T = sb("xn2T", [P, 2, CHUNK])

        logit = sb("logit", [P, E, NT])
        rest = sb("rest", [P, E, NT])
        top = sb("top", [P, 2, NT])
        same = sb("same", [P, E, NT])
        key = sb("key", [P, E, NT])
        pick = sb("pick", [P, 2, NT])
        hot = sb("hot", [P, 2, E, NT], BF16)
        dl = sb("dl", [P, E, NT])
        el = sb("el", [P, E, NT])
        d2 = sb("d2", [P, NT])
        e2 = sb("e2", [P, NT])
        den = sb("den", [P, NT])
        upto = sb("upto", [P, 2, E, NT])
        less = sb("less", [P, 2, E, NT])
        over = sb("over", [P, 2, E, NT])
        ntile = sb("ntile", [P, 2, E])
        cum = sb("cum", [P, 2, E])
        base = sb("base", [P, 2, E])
        place = sb("place", [P, 2, E, NT])
        pos1 = sb("pos1", [P, NT], I32)
        done_e = sb("done_e", [1, 2, SLOT_TILES, E])
        eid_f = sb("eid_f", [1, 2, SLOT_TILES])
        eid = sb("eid", [1, 2, SLOT_TILES], I32)

        rows2 = sb("rows2", [P, SLOT_TILES, ROW2])
        xs = sb("xs", [P, 2, C])
        w1s = sb("w1s", [P, 2, H + HC])
        xT = sb("xT", [P, 2, P])
        hT = sb("hT", [P, 2, H])
        res = sb("res", [P, 4, C])
        st2 = sb("st2", [P, 2, 4, 6])
        mv2 = sb("mv2", [P, 2, 4, 2])
        sd = sb("sd", [P, 2, 4])
        rs2 = sb("rs2", [P, 2, 4])
        tg = wkv[:, 0].rearrange("p (f c) -> p f c", c=C)
        zz = wkv[:, 1].rearrange("p (f c) -> p f c", c=C)
        yy = yq[:, 0].rearrange("p (f c) -> p f c", c=C)
        fin = yq[:, 1].rearrange("p (f c) -> p f c", c=C)
        ln_eps = sb("ln_eps", [P, 1])

        CONSTS = 21
        s_x = [sem(f"x_in{q}") for q in range(NQ)]
        s_wnat = sem("wnat_in")
        s_small = sem("small_in")
        s_moe = sem("expert_weights_in")
        s_const = sem("consts")
        s_fill = sem("fill_ready")
        s_filled1 = sem("sorted1_filled")
        s_filled2 = sem("sorted2_filled")
        s_wtps = sem("wT_psum")
        s_wt = sem("wT_ready")
        s_b1ps = sem("b1_psum")
        s_b1 = sem("b1_ready")
        s_par = sem("params")
        s_rest = sem("mix_rest_ready")
        s_st = sem("stats")
        s_mv = sem("moments")
        s_ve = sem("var_eps")
        s_rs = sem("rstd")
        s_xn = sem("xn")
        s_xtps = sem("xnT_psum")
        s_xt = sem("xnT")
        s_xm = sem("xm")
        s_kps = sem("k_psum")
        s_vps = sem("v_psum")
        s_rps = sem("r_psum")
        s_kc = sem("k_clamped")
        s_ke = sem("k_exp")
        s_th = sem("tanh")
        s_uk = sem("uk")
        s_kv = sem("kv")
        s_sk = sem("scan_k")
        s_skv = sem("scan_kv")
        s_wkv = sem("wkv")
        s_wks = sem("wk_sum")
        s_sg = sem("sigmoid")
        s_rec = sem("recip")
        s_yq = sem("quotient")
        s_rw = sem("rwkv")
        s_ops = sem("o_psum")
        s_on = sem("o_normed")
        s_x1 = sem("x1")
        s_x2 = sem("xn2")
        s_x2ps = sem("xn2T_psum")
        s_x2t = sem("xn2T")
        s_gps = sem("gate_psum")
        s_r = sem("route_steps")
        s_hot = sem("onehots")
        s_cnt = sem("counts_psum")
        s_dl = sem("gate_shifted")
        s_el = sem("gate_exp")
        s_pos = sem("positions")
        s_eid = sem("expert_ids")
        s_sc1 = sem("scatter1")
        s_in2 = [sem(f"rows2_in{i}") for i in range(4)]
        s_sc2 = sem("scatter2")
        s_in3 = [sem(f"rows3_in{i}") for i in range(4)]
        s_out = [sem(f"out_rows{f}") for f in range(4)]
        s_w1s = sem("w1_staged")
        s_xs = sem("xs")
        s_tps = sem("xsT_psum")
        s_tsb = sem("xsT")
        s_hps = sem("h_psum")
        s_h = sem("h")
        s_eps = sem("expert_psum")
        s_row = sem("row2_written")
        s_res = sem("res")
        s_f = [sem(f"final{i}") for i in range(12)]

        psX = bank[0]
        psT = [bank[0], bank[1]]
        psK, psV, psR = bank[2], bank[3], bank[4]
        psO = [bank[1], bank[5]]
        psX2 = bank[6]
        psG = bank[7]
        psC = bank[2]
        psH = [bank[2], bank[3]]
        psE = [bank[5], bank[6]]

        GROUPS = [(0, 4), (4, 10), (10, 16), (16, SLOT_TILES)]

        def group_of(s):
            return next(g for g, (a, b) in enumerate(GROUPS) if a <= s < b)

        block = ctx.enter_context(nc.Block())

        def pipeline(stages):
            last = NQ + max(lag for lag, _ in stages)
            for k in range(last):
                for lag, do in sorted(stages, key=lambda s: -s[0]):
                    if 0 <= k - lag < NQ:
                        do(k - lag)

        MV_ORDER = []
        pipeline([(lag, lambda q, n=n: MV_ORDER.append((n, q))) for n, lag in ((0, 0), (1, 6), (2, 7))])

        def mv_count(n, q):
            return MV_ORDER.index((n, q)) + 1

        RS_ORDER = []
        pipeline([(lag, lambda q, n=n: RS_ORDER.append((n, q))) for n, lag in ((0, 0), (1, 6), (2, 7))])

        def rs_count(n, q):
            return RS_ORDER.index((n, q)) + 1

        @block.sync
        def _(sp):
            for q in range(NQ):
                sp.dma_start(xin[:, q * TPC:(q + 1) * TPC, :],
                             xt_dram[:, q * TPC:(q + 1) * TPC, :]).then_inc(s_x[q], 16)
            sp.dma_start(w1_all[:, :, 0:H], w1.rearrange("e c h -> c e h")).then_inc(s_moe, 16)
            sp.dma_start(w2_all[:], w2.rearrange("e (j p) d -> p (e j) d", p=P)).then_inc(s_moe, 16)
            sp.dma_start(b1_rows[:], b1.rearrange("e (j p) -> (e j) p", p=P)).then_inc(s_moe, 16)
            sp.dma_start(b2_row[:], b2.rearrange("(a e) d -> a (e d)", a=1)).then_inc(s_moe, 16)
            sp.wait_ge(s_fill, 2)
            sp.dma_start(s1_tiles, fill[:, None, 2 * C:].to_broadcast([P, SLOT_TILES, ROW1])).then_inc(s_filled1, 16)
            sp.dma_start(s2_tiles, fill[:, None, :].to_broadcast([P, SLOT_TILES, ROW2])).then_inc(s_filled2, 16)
            sp.wait_ge(s_sc1, 16 * NT)
            for g, (a, b) in enumerate(GROUPS):
                sp.dma_start(rows2[:, a:b, 2 * C:], s1_tiles[:, a:b, :]).then_inc(s_in2[g], 16)
            sp.wait_ge(s_sc2, 16 * SLOT_TILES)
            for g, (a, b) in enumerate(GROUPS):
                sp.dma_start(rows3[:, a:b, :], s2_tiles[:, a:b, :]).then_inc(s_in3[g], 16)
            for f in range(4):
                sp.wait_ge(s_out[f], 16 * len(range(f, SLOT_TILES, 4)))

        @block.gpsimd
        def _(pool):
            g = nc.gpsimd
            g.memset(ident[:], 0.0).then_inc(s_const, 1)
            g.memset(before[:], 0.0).then_inc(s_const, 1)
            g.memset(minus_half[:], -0.5).then_inc(s_const, 1)
            pool.wait_ge(s_const, 2)
            g.affine_select(out=ident[:], in_=ident[:], compare_op=ALU.not_equal, fill=1.0, base=0,
                            pattern=[[-1, P]], channel_multiplier=1).then_inc(s_const, 1)
            g.affine_select(out=before[:], in_=before[:], compare_op=ALU.is_ge, fill=1.0, base=0,
                            pattern=[[-1, P]], channel_multiplier=1).then_inc(s_const, 1)
            g.memset(xnT[:, :, 0:1], 0.0).then_inc(s_const, 1)
            g.memset(sum_k[:, :, 0:1], 0.0).then_inc(s_const, 1)
            g.memset(sum_kv[:, :, 0:1], 0.0).then_inc(s_const, 1)
            g.memset(wk_eps[:], WK_EPS).then_inc(s_const, 1)
            g.memset(ln_eps[:], LN_EPS).then_inc(s_const, 1)
            g.memset(ones_b[:], 1.0).then_inc(s_const, 1)
            g.memset(ones_row[:], 1.0).then_inc(s_const, 1)
            g.memset(tile_keep[:], 1.0).then_inc(s_const, 1)
            g.memset(keep_e[:], 1.0).then_inc(s_const, 1)
            pool.wait_ge(s_const, 14)
            g.memset(tile_keep[:, :, :, 0:1], 0.0).then_inc(s_const, 1)
            g.memset(keep_e[:, :, 0:1], 0.0).then_inc(s_const, 1)
            g.iota(e_minus[:], pattern=[[1, E], [0, NT]], base=-E, channel_multiplier=0,
                   allow_small_or_imprecise_dtypes=True).then_inc(s_const, 1)
            g.iota(tile_start[:], pattern=[[0, 2 * E], [P, NT]], base=0, channel_multiplier=0,
                   allow_small_or_imprecise_dtypes=True).then_inc(s_const, 1)
            g.iota(slot_tile[:], pattern=[[0, 2], [1, SLOT_TILES], [0, E]], base=0, channel_multiplier=0,
                   allow_small_or_imprecise_dtypes=True).then_inc(s_const, 1)
            g.iota(rows1[:, :, C + A_TOK:C + A_TOK + 1].bitcast(I32), pattern=[[P, NT], [1, 1]], base=0,
                   channel_multiplier=1).then_inc(s_const, 1)
            g.memset(rows1[:, :, C + A_TOK + 1:], 0.0).then_inc(s_const, 1)
            g.memset(fill[:], 0.0).then_inc(s_fill, 1)
            pool.wait_ge(s_fill, 1)
            g.memset(fill[:, 2 * C + C + A_POS2:2 * C + C + A_TOK + 1].bitcast(I32), FILL).then_inc(s_fill, 1)

            def rstd(n, q):
                t = slice(q * TPC, (q + 1) * TPC)
                pool.wait_ge(s_mv, mv_count(n, q))
                g.tensor_scalar(veps[:, n, t], mv[:, n, t, 1], LN_EPS, None, ALU.add).then_inc(s_ve, 1)
                rstd.count += 1
                pool.wait_ge(s_ve, rstd.count)
                g.tensor_tensor(rs[:, n, t], veps[:, n, t], minus_half[:, t], ALU.pow).then_inc(s_rs, 1)

            rstd.count = 0

            def wk_sum(q):
                b, c, o = q // QPB, q % 2, (q % QPB) * CHUNK
                pool.wait_ge(s_uk, q + 1)
                pool.wait_ge(s_sk, q + 1)
                if q >= 2:
                    pool.wait_ge(s_rec, q - 1)
                g.tensor_tensor(wks[:, c], uk[:, c], sum_k[:, b, o:o + CHUNK], ALU.add).then_inc(s_wks, 1)
                pool.wait_ge(s_th, q + 1)
                g.tensor_scalar(sg[:, c], th[:, c], 0.5, 0.5, ALU.mult, ALU.add).then_inc(s_sg, 1)

            def rwkv(q):
                c = q % 2
                pool.wait_ge(s_wkv, q + 1)
                pool.wait_ge(s_rec, q + 1)
                g.tensor_tensor(yq[:, c], wkv[:, c], rec[:, c], ALU.mult).then_inc(s_yq, 1)
                pool.wait_ge(s_yq, q + 1)
                pool.wait_ge(s_sg, q + 1)
                if q >= 2:
                    pool.wait_ge(s_ops, q - 1)
                g.tensor_tensor(rw[:, c], yq[:, c], sg[:, c], ALU.mult).then_inc(s_rw, 1)

            pipeline([(0, lambda q: rstd(0, q)), (4, wk_sum), (5, rwkv),
                      (6, lambda q: rstd(1, q)), (7, lambda q: rstd(2, q))])

            pool.wait_ge(s_pos, 2)
            pool.wait_ge(s_filled1, 16)
            for i in range(NT):
                g.indirect_dma_start(sorted1, bass.IndirectOffsetOnAxis(ap=pos1[:, i:i + 1], axis=0),
                                     rows1[:, i, :], None).then_inc(s_sc1, 16)
            pool.wait_ge(s_filled2, 16)
            for s in range(SLOT_TILES):
                pool.wait_ge(s_row, s + 1)
                at = 3 * C + A_POS2
                g.indirect_dma_start(sorted2, bass.IndirectOffsetOnAxis(ap=rows2[:, s, at:at + 1].bitcast(I32), axis=0),
                                     rows2[:, s, :], None, bounds_check=SLOTS - 1, oob_is_err=False).then_inc(s_sc2, 16)
            for s in range(SLOT_TILES):
                f = s % 4
                pool.wait_ge(s_f[8], s + 1)
                if s >= 4:
                    pool.wait_ge(s_out[f], 16 * (s // 4))
                g.tensor_tensor(fin[:, f], yy[:, f], rows3[:, s, 2 * C:3 * C], ALU.add).then_inc(s_f[9], 1)
                pool.wait_ge(s_f[9], s + 1)
                at = 3 * C + A_TOK
                g.indirect_dma_start(out_rows, bass.IndirectOffsetOnAxis(ap=rows3[:, s, at:at + 1].bitcast(I32), axis=0),
                                     fin[:, f, :], None, bounds_check=TOKENS - 1, oob_is_err=False).then_inc(s_out[f], 16)

        @block.scalar
        def _(act):
            a = nc.scalar
            for n, w in enumerate((wk, wv, wr, wo)):
                act.dma_start(wnat[:, n, :], w).then_inc(s_wnat, 16)
            act.dma_start(mix[:], time_mix.rearrange("a b c -> c (a b)")).then_inc(s_small, 16)
            act.dma_start(decay_in[:], time_decay).then_inc(s_small, 16)
            act.dma_start(first_in[:], time_first).then_inc(s_small, 16)
            act.dma_start(gw[:], gate_w).then_inc(s_small, 16)
            act.dma_start(gb[:], gate_b[None, :].to_broadcast([P, E])).then_inc(s_small, 16)
            act.dma_start(gamma[:], ln_gamma[None, :].to_broadcast([P, C])).then_inc(s_small, 16)
            act.dma_start(beta[:], ln_beta[None, :].to_broadcast([P, C])).then_inc(s_small, 16)
            act.wait_ge(s_small, 16 * 7)
            a.activation(decay_e[:], decay_in[:], ACT.Exp).then_inc(s_par, 1)
            act.wait_ge(s_par, 1)
            a.activation(decay[:], decay_e[:], ACT.Exp, scale=-1.0).then_inc(s_par, 1)
            a.activation(first[:], first_in[:], ACT.Exp).then_inc(s_par, 1)
            act.wait_ge(s_par, 3)
            act.wait_ge(s_const, CONSTS)
            act.wait_ge(s_wtps, 1)
            a.activation(wT[:].rearrange("p n c -> p (n c)"), bank[0][:], ACT.Copy).then_inc(s_wt, 1)
            act.wait_ge(s_b1ps, 1)
            a.activation(w1_all[:, :, H:], bank[1][:, 0:E * HC].rearrange("p (e j) -> p e j", j=HC),
                         ACT.Copy).then_inc(s_b1, 1)

            def xnt(q):
                b, c, o = q // QPB, q % 2, (q % QPB) * CHUNK
                act.wait_ge(s_xtps, q + 1)
                a.activation(xnT[:, b, 1 + o:1 + o + CHUNK], psX[:], ACT.Copy)
                if q >= 2:
                    act.wait_ge(s_xm, q - 1)
                a.activation(xmix[:, c], psX[:], ACT.Copy, scale=mix[:, 0:1]).then_inc(s_xt, 1)

            def kexp(q):
                c = q % 2
                act.wait_ge(s_kc, q + 1)
                if q >= 2:
                    act.wait_ge(s_kv, q - 1)
                    act.wait_ge(s_sk, q - 1)
                a.activation(ke[:, c], kc[:, c], ACT.Exp).then_inc(s_ke, 1)

            def sigmoid_uk(q):
                c = q % 2
                act.wait_ge(s_rps, q + 1)
                if q >= 2:
                    act.wait_ge(s_sg, q - 1)
                a.activation(th[:, c], psR[:], ACT.Tanh, scale=0.5).then_inc(s_th, 1)
                act.wait_ge(s_ke, q + 1)
                if q >= 2:
                    act.wait_ge(s_wks, q - 1)
                a.activation(uk[:, c], ke[:, c], ACT.Identity, bias=wk_eps[:, 0:1], scale=first[:, 0:1]).then_inc(s_uk, 1)

            def xn2t(q):
                act.wait_ge(s_x2ps, q + 1)
                if q >= 2:
                    act.wait_ge(s_gps, q - 1)
                a.activation(xn2T[:, q % 2], psX2[:], ACT.Copy).then_inc(s_x2t, 1)

            pipeline([(1, xnt), (3, kexp), (4, sigmoid_uk), (8, xn2t)])

            act.wait_ge(s_dl, 2)
            a.activation(el[:], dl[:], ACT.Exp).then_inc(s_el, 1)
            a.activation(e2[:], d2[:], ACT.Exp).then_inc(s_el, 1)

            def xT_copy(n):
                act.wait_ge(s_tps, n + 1)
                if n >= 2:
                    act.wait_ge(s_hps, n - 1)
                a.activation(xT[:, n % 2], psT[n % 2][:, 0:P], ACT.Copy).then_inc(s_tsb, 1)

            def relu(n):
                act.wait_ge(s_hps, n + 1)
                if n >= 2:
                    act.wait_ge(s_eps, n - 1)
                for j in range(HC):
                    ins = a.activation(hT[:, n % 2, j * P:(j + 1) * P], psH[n % 2][:, j * P:(j + 1) * P],
                                       ACT.Relu, bias=w1s[:, n % 2, H + j:H + j + 1])
                ins.then_inc(s_h, 1)

            def root(s, stage, src, want):
                act.wait_ge(want, s + 1)
                a.activation(sd[:, stage, s % 4:s % 4 + 1], mv2[:, stage, s % 4, 1:2], ACT.Sqrt,
                             bias=ln_eps[:, 0:1]).then_inc(s_f[src], 1)

            for k in range(SLOT_TILES + 2):
                if 1 <= k <= SLOT_TILES:
                    relu(k - 1)
                if k < SLOT_TILES:
                    xT_copy(k)
            for k in range(SLOT_TILES + 6):
                if 4 <= k < SLOT_TILES + 4:
                    root(k - 4, 1, 5, s_f[4])
                if 3 <= k < SLOT_TILES + 3:
                    root(k - 3, 0, 1, s_f[0])
                if 1 <= k <= SLOT_TILES:
                    relu(SLOT_TILES + k - 1)
                if k < SLOT_TILES:
                    xT_copy(SLOT_TILES + k)

        @block.tensor
        def _(pe):
            t = nc.tensor
            pe.wait_ge(s_const, CONSTS)
            pe.wait_ge(s_wnat, 64)
            for n in range(4):
                ins = t.transpose(bank[0][:, n * C:(n + 1) * C], wnat[:, n, :], ident[:])
            ins.then_inc(s_wtps, 1)
            pe.wait_ge(s_moe, 64)
            t.transpose(bank[1][:, 0:E * HC], b1_rows[:], ident[0:E * HC, 0:E * HC]).then_inc(s_b1ps, 1)

            def transpose_xn(q):
                pe.wait_ge(s_xn, q + 1)
                pe.wait_ge(s_wt, 1)
                if q >= 1:
                    pe.wait_ge(s_xt, q)
                for i in range(TPC):
                    ins = t.transpose(psX[:, i * P:(i + 1) * P], xn[:, q * TPC + i, :], ident[:])
                ins.then_inc(s_xtps, 1)

            def project_k(q):
                pe.wait_ge(s_xm, q + 1)
                if q >= 1:
                    pe.wait_ge(s_kc, q)
                t.matmul(psK[:], wT[:, 0, :], xm[:, q % 3], start=True, stop=True).then_inc(s_kps, 1)

            def project_vr(q):
                if q >= 1:
                    pe.wait_ge(s_kv, q)
                t.matmul(psV[:], wT[:, 1, :], xm[:, q % 3], start=True, stop=True).then_inc(s_vps, 1)
                if q >= 1:
                    pe.wait_ge(s_th, q)
                t.matmul(psR[:], wT[:, 2, :], xm[:, q % 3], start=True, stop=True).then_inc(s_rps, 1)

            def output(q):
                pe.wait_ge(s_rw, q + 1)
                if q >= 2:
                    pe.wait_ge(s_on, q - 1)
                if q == 0:
                    pe.wait_ge(s_b1, 1)
                for i in range(TPC):
                    ins = t.matmul(psO[q % 2][:, i * P:(i + 1) * P], rw[:, q % 2, i * P:(i + 1) * P], wT[:, 3, :],
                                   start=True, stop=True)
                ins.then_inc(s_ops, 1)

            def transpose_x2(q):
                pe.wait_ge(s_x2, q + 1)
                if q >= 1:
                    pe.wait_ge(s_x2t, q)
                for i in range(TPC):
                    ins = t.transpose(psX2[:, i * P:(i + 1) * P], xn[:, q * TPC + i, :], ident[:])
                ins.then_inc(s_x2ps, 1)

            def gate(q):
                pe.wait_ge(s_x2t, q + 1)
                for i in range(TPC):
                    n = q * TPC + i
                    ins = t.matmul(psG[:, n * E:(n + 1) * E], xn2T[:, q % 2, i * P:(i + 1) * P], gw[:],
                                   start=True, stop=True)
                ins.then_inc(s_gps, 1)

            pipeline([(1, transpose_xn), (3, project_k), (4, project_vr), (6, output), (8, transpose_x2), (9, gate)])

            pe.wait_ge(s_hot, 2)
            hots = hot[:].rearrange("p r e n -> p (r e n)")
            t.matmul(psC[:, 0:256], before[:], hots, start=True, stop=True)
            t.matmul(psC[:, 256:512], ones_b[:], hots, start=True, stop=True).then_inc(s_cnt, 1)

            def turn(n):
                s = n % SLOT_TILES
                if n < SLOT_TILES:
                    pe.wait_ge(s_xs, n + 1)
                    src = xs[:, n % 2, :]
                else:
                    pe.wait_ge(s_in3[group_of(s)], 16)
                    src = rows3[:, s, 0:C]
                if n >= 2:
                    pe.wait_ge(s_tsb, n - 1)
                t.transpose(psT[n % 2][:, 0:P], src, ident[:]).then_inc(s_tps, 1)

            def hidden(n):
                pe.wait_ge(s_tsb, n + 1)
                pe.wait_ge(s_w1s, n + 1)
                if n >= 2:
                    pe.wait_ge(s_h, n - 1)
                if n == 0:
                    pe.wait_ge(s_eid, 1)
                for j in range(HC):
                    ins = t.matmul(psH[n % 2][:, j * P:(j + 1) * P], w1s[:, n % 2, j * P:(j + 1) * P],
                                   xT[:, n % 2], start=True, stop=True)
                ins.then_inc(s_hps, 1)

            def second(n):
                r, s = divmod(n, SLOT_TILES)
                e = pe.value_load(eid[0:1, r, s:s + 1], min_val=0, max_val=E - 1)
                pe.wait_ge(s_h, n + 1)
                if n >= 2:
                    pe.wait_ge(s_row if n < SLOT_TILES + 2 else s_res, n - 1 if n < SLOT_TILES + 2 else n - 1 - SLOT_TILES)
                w2f = w2_all[:].rearrange("p a d -> p (a d)")
                for j in range(HC):
                    t.matmul(psE[n % 2][:, 0:C], hT[:, n % 2, j * P:(j + 1) * P],
                             w2f[:, bass.ds(e * (HC * C) + j * C, C)], start=(j == 0), stop=False)
                t.matmul(psE[n % 2][:, 0:C], ones_row[:], b2_row[:, bass.ds(e * C, C)],
                         start=False, stop=True).then_inc(s_eps, 1)

            for r in range(2):
                for k in range(SLOT_TILES + 2):
                    n = r * SLOT_TILES + k
                    if 2 <= k:
                        second(n - 2)
                    if 1 <= k <= SLOT_TILES:
                        hidden(n - 1)
                    if k < SLOT_TILES:
                        turn(n)

        @block.vector
        def _(dve):
            v = nc.vector
            dve.wait_ge(s_small, 16 * 7)
            v.tensor_scalar(mix_rest[:], mix[:], -1.0, 1.0, ALU.mult, ALU.add).then_inc(s_rest, 1)

            def moments(n, q, src):
                for i in range(TPC):
                    v_ = v.bn_stats(st[:, n, q * TPC + i, :], src(i))
                v_.then_inc(s_st, 1)
                moments.count += 1
                dve.wait_ge(s_st, moments.count)
                for i in range(TPC):
                    v_ = v.bn_aggr(mv[:, n, q * TPC + i, :], st[:, n, q * TPC + i, :])
                v_.then_inc(s_mv, 1)

            moments.count = 0

            def stats_x(q):
                dve.wait_ge(s_x[q], 16)
                moments(0, q, lambda i: xin[:, q * TPC + i, :])

            def norm_x(q):
                dve.wait_ge(s_rs, rs_count(0, q))
                for i in range(q * TPC, (q + 1) * TPC):
                    v_ = v.tensor_scalar(xn[:, i, :], xin[:, i, :], mv[:, 0, i, 0:1], rs[:, 0, i:i + 1],
                                         ALU.subtract, ALU.mult)
                v_.then_inc(s_xn, 1)

            def mix_x(q):
                b, c, o = q // QPB, q % 2, (q % QPB) * CHUNK
                dve.wait_ge(s_xt, q + 1)
                if q == 0:
                    dve.wait_ge(s_rest, 1)
                    dve.wait_ge(s_par, 3)
                    dve.wait_ge(s_const, CONSTS)
                if q >= 3:
                    dve.wait_ge(s_rps, q - 2)
                v.scalar_tensor_tensor(xm[:, q % 3], xnT[:, b, o:o + CHUNK], mix_rest[:, 0:1], xmix[:, c],
                                       ALU.mult, ALU.add).then_inc(s_xm, 1)

            def clamp_k(q):
                dve.wait_ge(s_kps, q + 1)
                if q >= 2:
                    dve.wait_ge(s_ke, q - 1)
                v.tensor_scalar(kc[:, q % 2], psK[:], K_MAX, None, ALU.min).then_inc(s_kc, 1)

            def scans(q):
                b, c, o = q // QPB, q % 2, (q % QPB) * CHUNK
                dve.wait_ge(s_ke, q + 1)
                dve.wait_ge(s_vps, q + 1)
                v.tensor_tensor(kv[:, c], ke[:, c], psV[:], ALU.mult).then_inc(s_kv, 1)
                lam = decay[:, 0:1].to_broadcast([P, CHUNK])
                if q >= 1:
                    dve.wait_ge(s_skv, q)
                v.tensor_tensor_scan(sum_k[:, b, 1 + o:1 + o + CHUNK], lam, ke[:, c],
                                     sum_k[:, b, o:o + 1], ALU.mult, ALU.add).then_inc(s_sk, 1)
                dve.wait_ge(s_kv, q + 1)
                v.tensor_tensor_scan(sum_kv[:, b, 1 + o:1 + o + CHUNK], lam, kv[:, c],
                                     sum_kv[:, b, o:o + 1], ALU.mult, ALU.add).then_inc(s_skv, 1)

            def quotient(q):
                b, c, o = q // QPB, q % 2, (q % QPB) * CHUNK
                dve.wait_ge(s_skv, q + 1)
                if q >= 2:
                    dve.wait_ge(s_yq, q - 1)
                v.scalar_tensor_tensor(wkv[:, c], kv[:, c], first[:, 0:1], sum_kv[:, b, o:o + CHUNK],
                                       ALU.mult, ALU.add).then_inc(s_wkv, 1)
                dve.wait_ge(s_wks, q + 1)
                v.reciprocal(rec[:, c], wks[:, c]).then_inc(s_rec, 1)

            def stats_o(q):
                dve.wait_ge(s_ops, q + 1)
                moments(1, q, lambda i: psO[q % 2][:, i * P:(i + 1) * P])

            def residual(q):
                dve.wait_ge(s_rs, rs_count(1, q))
                for i in range(TPC):
                    n = q * TPC + i
                    v_ = v.tensor_scalar(on[:, q % 2, i, :], psO[q % 2][:, i * P:(i + 1) * P], mv[:, 1, n, 0:1],
                                         rs[:, 1, n:n + 1], ALU.subtract, ALU.mult)
                v_.then_inc(s_on, 1)
                dve.wait_ge(s_on, q + 1)
                v.tensor_tensor(rows1[:, q * TPC:(q + 1) * TPC, 0:C], on[:, q % 2],
                                xin[:, q * TPC:(q + 1) * TPC, :], ALU.add).then_inc(s_x1, 1)
                dve.wait_ge(s_x1, q + 1)
                moments(2, q, lambda i: rows1[:, q * TPC + i, 0:C])

            def norm_x1(q):
                dve.wait_ge(s_rs, rs_count(2, q))
                dve.wait_ge(s_xtps, q + 1)
                for i in range(q * TPC, (q + 1) * TPC):
                    v_ = v.tensor_scalar(xn[:, i, :], rows1[:, i, 0:C], mv[:, 2, i, 0:1], rs[:, 2, i:i + 1],
                                         ALU.subtract, ALU.mult)
                v_.then_inc(s_x2, 1)

            pipeline([(0, stats_x), (1, norm_x), (2, mix_x), (3, clamp_k), (4, scans),
                      (5, quotient), (6, stats_o), (7, residual), (8, norm_x1)])

            def by_tile(ap):
                return ap.rearrange("p e n -> p n e")

            def per_expert(ap):
                return ap[:, None, :].to_broadcast([P, E, NT])

            count = [0]

            def step(ins):
                ins.then_inc(s_r, 1)
                count[0] += 1
                dve.wait_ge(s_r, count[0])

            dve.wait_ge(s_gps, NQ)
            step(v.tensor_tensor(logit[:], psG[:, 0:NT * E].rearrange("p (n e) -> p e n", e=E),
                                 gb[:, :, None].to_broadcast([P, E, NT]), ALU.add))
            for r, src in ((0, logit), (1, rest)):
                step(v.tensor_reduce(top[:, r, :], by_tile(src[:]), AXX, ALU.max))
                step(v.tensor_tensor(same[:], src[:], per_expert(top[:, r, :]), ALU.is_equal))
                step(v.tensor_tensor(key[:], same[:], e_minus[:], ALU.mult))
                step(v.tensor_reduce(pick[:, r, :], by_tile(key[:]), AXX, ALU.min))
                ins = v.tensor_tensor(hot[:, r], e_minus[:], per_expert(pick[:, r, :]), ALU.is_equal)
                ins.then_inc(s_hot, 1)
                dve.wait_ge(s_hot, r + 1)
                if r == 0:
                    step(v.scalar_tensor_tensor(rest[:], hot[:, 0], -BIG, logit[:], ALU.mult, ALU.add))
            v.tensor_tensor(dl[:], logit[:], per_expert(top[:, 0, :]), ALU.subtract).then_inc(s_dl, 1)
            v.tensor_tensor(d2[:], top[:, 1, :], top[:, 0, :], ALU.subtract).then_inc(s_dl, 1)

            dve.wait_ge(s_cnt, 1)
            totals = psC[:, 256:512]
            flat = lambda ap: ap.rearrange("p r e n -> p (r e n)")
            step(v.tensor_tensor_scan(flat(upto[:]), flat(tile_keep[:]), totals, 0.0, ALU.mult, ALU.add))
            counts = upto[:, :, :, NT - 1:NT].to_broadcast([P, 2, E, NT])
            v.tensor_tensor(flat(less[:]), flat(upto[:]), totals, ALU.subtract).then_inc(s_r, 1)
            count[0] += 1
            step(v.tensor_tensor(over[:], counts, tile_start[:], ALU.is_gt))
            step(v.tensor_reduce(ntile[:], over[:], AXX, ALU.add))
            step(v.tensor_tensor_scan(cum[:].rearrange("p r e -> p (r e)"), keep_e[:].rearrange("p r e -> p (r e)"),
                                      ntile[:].rearrange("p r e -> p (r e)"), 0.0, ALU.mult, ALU.add))
            step(v.tensor_tensor(base[:], cum[:], ntile[:], ALU.subtract))
            step(v.tensor_tensor(flat(place[:]), flat(less[:]), psC[:, 0:256], ALU.add))
            step(v.scalar_tensor_tensor(less[:].rearrange("p r e n -> p (r e) n"),
                                        base[:].rearrange("p r e -> p (r e)")[:, :, None].to_broadcast([P, 2 * E, NT]),
                                        float(P), place[:].rearrange("p r e n -> p (r e) n"), ALU.mult, ALU.add))
            step(v.tensor_tensor(place[:], less[:], hot[:], ALU.mult))
            with nc.allow_low_precision(reason="slots are whole numbers far below 2 ** 24"):
                v.tensor_reduce(pos1[:], by_tile(place[:, 0]), AXX, ALU.add).then_inc(s_r, 1)
                v.tensor_reduce(rows1[:, :, C + A_POS2].bitcast(I32), by_tile(place[:, 1]), AXX,
                                ALU.add).then_inc(s_r, 1)
            count[0] += 2
            dve.wait_ge(s_el, 2)
            step(v.tensor_reduce(den[:], by_tile(el[:]), AXX, ALU.add))
            step(v.reciprocal(rows1[:, :, C + A_G0], den[:]))
            v.tensor_tensor(rows1[:, :, C + A_G1], e2[:], rows1[:, :, C + A_G0], ALU.mult)
            v.tensor_copy(rows1[:, :, C + A_MEAN], mv[:, 2, :, 0])
            v.tensor_copy(rows1[:, :, C + A_RSTD], rs[:, 2, :]).then_inc(s_pos, 2)
            step(v.tensor_tensor(done_e[:], cum[0:1, :, None, :].to_broadcast([1, 2, SLOT_TILES, E]),
                                 slot_tile[:], ALU.is_le))
            step(v.tensor_reduce(eid_f[:], done_e[:], AXX, ALU.add))
            v.tensor_scalar(eid[:], eid_f[:], float(E - 1), None, ALU.min).then_inc(s_eid, 1)
            dve.wait_ge(s_eid, 1)

            w1f = w1_all[:].rearrange("p e h -> p (e h)")

            def stage_w1(n):
                r, s = divmod(n, SLOT_TILES)
                e = dve.value_load(eid[0:1, r, s:s + 1], min_val=0, max_val=E - 1)
                if n >= 2:
                    dve.wait_ge(s_h, n - 1)
                v.tensor_copy(w1s[:, n % 2, :], w1f[:, bass.ds(e * (H + HC), H + HC)]).then_inc(s_w1s, 1)

            def aux(rows, s, what):
                return rows[:, s, 3 * C + what:3 * C + what + 1]

            def norm_rows(s):
                dve.wait_ge(s_in2[group_of(s)], 16)
                if s >= 2:
                    dve.wait_ge(s_tps, s - 1)
                    dve.wait_ge(s_row, s - 1)
                v.tensor_scalar(xs[:, s % 2, :], rows2[:, s, 2 * C:3 * C], aux(rows2, s, A_MEAN),
                                aux(rows2, s, A_RSTD), ALU.subtract, ALU.mult).then_inc(s_xs, 1)

            def write_row(s):
                dve.wait_ge(s_eps, s + 1)
                v.scalar_tensor_tensor(rows2[:, s, 0:C], psE[s % 2][:, 0:C], ALPHA, xs[:, s % 2, :],
                                       ALU.mult, ALU.add)
                v.scalar_tensor_tensor(rows2[:, s, C:2 * C], psE[s % 2][:, 0:C], aux(rows2, s, A_G0),
                                       xs[:, s % 2, :], ALU.mult, ALU.add).then_inc(s_row, 1)

            for k in range(SLOT_TILES + 2):
                if k >= 2:
                    write_row(k - 2)
                if k < SLOT_TILES:
                    stage_w1(k)
                    norm_rows(k)

            def fuse(s):
                n = SLOT_TILES + s
                dve.wait_ge(s_eps, n + 1)
                dve.wait_ge(s_in3[group_of(s)], 16)
                v.scalar_tensor_tensor(res[:, s % 4], psE[n % 2][:, 0:C], aux(rows3, s, A_G1),
                                       rows3[:, s, C:2 * C], ALU.mult, ALU.add).then_inc(s_res, 1)
                dve.wait_ge(s_res, s + 1)
                v.bn_stats(st2[:, 0, s % 4, :], res[:, s % 4]).then_inc(s_f[10], 1)
                dve.wait_ge(s_f[10], s + 1)
                v.bn_aggr(mv2[:, 0, s % 4, :], st2[:, 0, s % 4, :]).then_inc(s_f[0], 1)

            def inner_norm(s):
                f = s % 4
                dve.wait_ge(s_f[1], s + 1)
                v.reciprocal(rs2[:, 0, f:f + 1], sd[:, 0, f:f + 1]).then_inc(s_f[2], 1)
                v.scalar_tensor_tensor(tg[:, f], res[:, f], mv2[:, 0, f, 0:1], gamma[:], ALU.subtract,
                                       ALU.mult).then_inc(s_f[2], 1)
                dve.wait_ge(s_f[2], 2 * s + 2)
                v.scalar_tensor_tensor(zz[:, f], tg[:, f], rs2[:, 0, f:f + 1], beta[:], ALU.mult,
                                       ALU.add).then_inc(s_f[3], 1)
                dve.wait_ge(s_f[3], s + 1)
                v.bn_stats(st2[:, 1, f, :], zz[:, f]).then_inc(s_f[11], 1)
                dve.wait_ge(s_f[11], s + 1)
                v.bn_aggr(mv2[:, 1, f, :], st2[:, 1, f, :]).then_inc(s_f[4], 1)

            def outer_norm(s):
                f = s % 4
                dve.wait_ge(s_f[5], s + 1)
                v.reciprocal(rs2[:, 1, f:f + 1], sd[:, 1, f:f + 1]).then_inc(s_f[6], 1)
                dve.wait_ge(s_f[6], s + 1)
                if s >= 4:
                    dve.wait_ge(s_f[9], s - 3)
                v.tensor_scalar(yy[:, f], zz[:, f], mv2[:, 1, f, 0:1], rs2[:, 1, f:f + 1], ALU.subtract,
                                ALU.mult).then_inc(s_f[8], 1)

            for k in range(SLOT_TILES + 6):
                if 5 <= k < SLOT_TILES + 5:
                    outer_norm(k - 5)
                if 4 <= k < SLOT_TILES + 4:
                    inner_norm(k - 4)
                if 3 <= k < SLOT_TILES + 3:
                    fuse(k - 3)
                if k < SLOT_TILES:
                    stage_w1(SLOT_TILES + k)


_INS = ['L0_attn_x', 'L0_attn_time_decay', 'L0_attn_time_first', 'L0_attn_time_mix', 'L0_attn_Wk',
        'L0_attn_Wv', 'L0_attn_Wr', 'L0_attn_Wo', 'L0_ffn_gate_W', 'L0_ffn_gate_b', 'L0_ffn_W1',
        'L0_ffn_b1', 'L0_ffn_W2', 'L0_ffn_b2', 'L0_ffn_ln_gamma', 'L0_ffn_ln_beta']


def kernel(**inputs):
    import numpy as np
    import concourse.bacc as bacc
    from concourse.bass_utils import run_bass_kernel_spmd as run

    nc = bacc.Bacc("TRN2", target_bir_lowering=False, num_devices=1)
    arrays, args = {}, []
    for name in _INS:
        a = np.ascontiguousarray(inputs[name])
        arrays[f"in_{name}"] = a
        args.append(nc.dram_tensor(f"in_{name}", a.shape, mybir.dt.from_np(a.dtype), kind="ExternalInput").ap())
    o = nc.dram_tensor("o", arrays["in_L0_attn_x"].shape, F32, kind="ExternalOutput").ap()
    build_program(nc, *args, o)
    r = run(nc, [arrays], core_ids=[0])
    return r.results[0]["o"]
```

```python
from contextlib import ExitStack

import concourse.bass as bass
from concourse import mybir

ALU = mybir.AluOpType
ACT = mybir.ActivationFunctionType
AXX = mybir.AxisListType.X
F32 = mybir.dt.float32
BF16 = mybir.dt.bfloat16
I32 = mybir.dt.int32

P = 128
LN_EPS = 1e-5
K_MAX = 60.0
WK_EPS = 1e-9
ALPHA = 0.5
CHUNK = 512
TPC = CHUNK // P
AUX = 8
A_MEAN, A_RSTD, A_G0, A_G1, A_POS2, A_TOK = range(6)
BIG = 3.0e38


def build_program(nc, x, time_decay, time_first, time_mix, wk, wv, wr, wo,
                  gate_w, gate_b, w1, b1, w2, b2, ln_gamma, ln_beta, out):
    B, T, C = x.shape
    E, _, H = w1.shape
    TOKENS = B * T
    NT = TOKENS // P
    NQ = TOKENS // CHUNK
    QPB = T // CHUNK
    HC = H // P
    SLOT_TILES = NT + E - 1
    SLOTS = SLOT_TILES * P
    ROW1 = C + AUX
    ROW2 = 2 * C + ROW1
    FILL = 1 << 20
    assert C == P and T % CHUNK == 0 and H == HC * P

    xt_dram = x.rearrange("b t c -> (b t) c").rearrange("(n p) c -> p n c", p=P)
    out_rows = out.rearrange("b t c -> (b t) c")
    sorted1 = nc.dram_tensor("sorted1", (SLOTS, ROW1), F32, kind="Internal").ap()
    sorted2 = nc.dram_tensor("sorted2", (SLOTS, ROW2), F32, kind="Internal").ap()
    s1_tiles = sorted1.rearrange("(s p) w -> p s w", p=P)
    s2_tiles = sorted2.rearrange("(s p) w -> p s w", p=P)

    with ExitStack() as ctx:
        def sb(name, shape, dt=F32):
            return ctx.enter_context(nc.sbuf_tensor(name, shape, dt))

        def sem(name):
            return ctx.enter_context(nc.semaphore(name))

        bank = [ctx.enter_context(nc.psum_tensor(f"bank{i}", [P, 512], F32)) for i in range(8)]

        wnat = sb("wnat", [P, 4, C])
        wT = sb("wT", [P, 4, C])
        decay_in = sb("decay_in", [P, 1])
        first_in = sb("first_in", [P, 1])
        mix = sb("mix", [P, 1])
        mix_rest = sb("mix_rest", [P, 1])
        decay_e = sb("decay_e", [P, 1])
        decay = sb("decay", [P, 1])
        first = sb("first", [P, 1])
        wk_eps = sb("wk_eps", [P, 1])
        gw = sb("gw", [P, E])
        gb = sb("gb", [P, E])
        w1_all = sb("w1_all", [P, E, H + HC])
        b1_rows = sb("b1_rows", [E * HC, P])
        w2_all = sb("w2_all", [P, E * HC, C])
        b2_rows = sb("b2_rows", [3, E * C])
        b2_part = sb("b2_part", [3, 2, E * C], BF16)
        b2_split = sb("b2_split", [3, E * C], BF16)
        gamma = sb("gamma", [P, C])
        beta = sb("beta", [P, C])
        ident = sb("ident", [P, P])
        before = sb("before", [P, P], BF16)
        ones_b = sb("ones_b", [P, P], BF16)
        ones_row = sb("ones_row", [3, P], BF16)
        minus_half = sb("minus_half", [P, NT])
        e_minus = sb("e_minus", [P, E, NT])
        tile_start = sb("tile_start", [P, 2, E, NT])
        slot_tile = sb("slot_tile", [1, 2, SLOT_TILES, E])
        tile_keep = sb("tile_keep", [P, 2, E, NT])
        keep_e = sb("keep_e", [P, 2, E])
        fill = sb("fill", [P, ROW2])

        rows2 = sb("rows2", [P, SLOT_TILES, ROW2])
        rows3 = sb("rows3", [P, SLOT_TILES, ROW2])
        taken = {"rows2": 0, "rows3": 0}

        def over(name, a, b):
            at = taken[name]
            taken[name] += a * b
            assert taken[name] <= SLOT_TILES * ROW2
            flat_rows = (rows2 if name == "rows2" else rows3)[:].rearrange("p s w -> p (s w)")
            return flat_rows[:, at:at + a * b].rearrange("p (a b) -> p a b", b=b)

        xin = sb("xin", [P, NT, C])
        st = sb("st", [P, 3, NT, 6])
        mv = sb("mv", [P, 3, NT, 2])
        veps = sb("veps", [P, 3, NT])
        rs = sb("rs", [P, 3, NT])
        xn = sb("xn", [P, NT, C])
        xnT = over("rows3", B, T + 1)
        xmix = over("rows3", 2, CHUNK)
        xm = over("rows3", 3, CHUNK)
        kc = over("rows3", 2, CHUNK)
        ke = over("rows2", 2, CHUNK)
        kv = over("rows3", 2, CHUNK)
        th = over("rows3", 2, CHUNK)
        sg = over("rows2", 2, CHUNK)
        uk = over("rows2", 2, CHUNK)
        sum_k = sb("sum_k", [P, B, T + 1])
        sum_kv = sb("sum_kv", [P, B, T + 1])
        wkv = sb("wkv", [P, 2, CHUNK])
        wks = over("rows2", 2, CHUNK)
        rec = over("rows2", 2, CHUNK)
        yq = sb("yq", [P, 2, CHUNK])
        rw = sb("rw", [P, 2, CHUNK])
        on = sb("on", [P, 2, TPC, C])
        rows1 = sb("rows1", [P, NT, ROW1])
        xn2T = over("rows2", 2, CHUNK)

        logit = sb("logit", [P, E, NT])
        rest = sb("rest", [P, E, NT])
        top = sb("top", [P, 2, NT])
        same = sb("same", [P, E, NT])
        key = sb("key", [P, E, NT])
        pick = sb("pick", [P, 2, NT])
        hot = sb("hot", [P, 2, E, NT], BF16)
        dl = sb("dl", [P, E, NT])
        el = sb("el", [P, E, NT])
        d2 = sb("d2", [P, NT])
        e2 = sb("e2", [P, NT])
        den = sb("den", [P, NT])
        upto = sb("upto", [P, 2, E, NT])
        less = sb("less", [P, 2, E, NT])
        longer = sb("longer", [P, 2, E, NT])
        ntile = sb("ntile", [P, 2, E])
        cum = sb("cum", [P, 2, E])
        base = sb("base", [P, 2, E])
        place = sb("place", [P, 2, E, NT])
        pos1 = sb("pos1", [P, NT], I32)
        done_e = sb("done_e", [1, 2, SLOT_TILES, E])
        eid_f = sb("eid_f", [1, 2, SLOT_TILES])
        eid = sb("eid", [1, 2, SLOT_TILES], I32)

        w1s = sb("w1s", [P, 4, H + HC])
        xT = sb("xT", [P, 2, P])
        hT = sb("hT", [P, 3, H])
        st2 = sb("st2", [P, 2, SLOT_TILES, 6])
        mv2 = sb("mv2", [P, 2, SLOT_TILES, 2])
        sd = sb("sd", [P, 2, SLOT_TILES])
        rs2 = sb("rs2", [P, 2, SLOT_TILES])
        shift = sb("shift", [P, SLOT_TILES])
        ln_eps = sb("ln_eps", [P, 1])

        CONSTS = 21
        s_x = [sem(f"x_in{q}") for q in range(NQ)]
        s_wnat = sem("wnat_in")
        s_small = sem("small_in")
        s_gate = sem("gate_in")
        s_w1 = sem("w1_in")
        s_w2 = sem("w2_in")
        s_moe = sem("b1_in")
        s_b2 = sem("b2_in")
        s_b2s = sem("b2_parts")
        s_norm = sem("norm_in")
        s_const = sem("consts")
        s_fill = sem("fill_ready")
        s_filled1 = sem("sorted1_filled")
        s_filled2 = sem("sorted2_filled")
        s_wtps = sem("wT_psum")
        s_wt = sem("wT_ready")
        s_b1ps = sem("b1_psum")
        s_b1 = sem("b1_ready")
        s_par = sem("params")
        s_rest = sem("mix_rest_ready")
        s_st = sem("stats")
        s_mv = sem("moments")
        s_ve = sem("var_eps")
        s_rs = sem("rstd")
        s_xn = sem("xn")
        s_xtps = sem("xnT_psum")
        s_xt = sem("xnT")
        s_xm = sem("xm")
        s_kps = sem("k_psum")
        s_vps = sem("v_psum")
        s_rps = sem("r_psum")
        s_kc = sem("k_clamped")
        s_ke = sem("k_exp")
        s_th = sem("tanh")
        s_uk = sem("uk")
        s_kv = sem("kv")
        s_sk = sem("scan_k")
        s_skv = sem("scan_kv")
        s_wkv = sem("wkv")
        s_wks = sem("wk_sum")
        s_sg = sem("sigmoid")
        s_rec = sem("recip")
        s_yq = sem("quotient")
        s_rw = sem("rwkv")
        s_ops = sem("o_psum")
        s_on = sem("o_normed")
        s_x1 = sem("x1")
        s_x2 = sem("xn2")
        s_x2ps = sem("xn2T_psum")
        s_x2t = sem("xn2T")
        s_gps = sem("gate_psum")
        s_r = sem("route_steps")
        s_hot = sem("onehots")
        s_cnt = sem("counts_psum")
        s_dl = sem("gate_shifted")
        s_el = sem("gate_exp")
        s_pos = sem("positions")
        s_eid = sem("expert_ids")
        s_sc1 = sem("scatter1")
        s_in2 = [sem(f"rows2_in{i}") for i in range(4)]
        s_sc2 = sem("scatter2")
        s_in3 = [sem(f"rows3_in{i}") for i in range(4)]
        s_out = sem("out_rows")
        s_w1s = sem("w1_staged")
        s_xs = sem("xs")
        s_tps = sem("xsT_psum")
        s_tsb = sem("xsT")
        s_hps = sem("h_psum")
        s_h = sem("h")
        s_eps = sem("expert_psum")
        s_row = sem("row2_written")
        s_res = sem("residual_sum")
        s_st2 = [sem("inner_stats"), sem("outer_stats")]
        s_mv2 = [sem("inner_moments"), sem("outer_moments")]
        s_sd = [sem("inner_deviation"), sem("outer_deviation")]
        s_rs2 = [sem("inner_rstd"), sem("outer_rstd")]
        s_tg = sem("times_gamma")
        s_zz = sem("inner_norm")
        s_shift = sem("outer_shift")
        s_yy = sem("outer_norm")
        s_fin = sem("row_finished")

        psX = bank[0]
        psT = [bank[0], bank[1]]
        psK, psV, psR = bank[2], bank[3], bank[4]
        psO = [bank[1], bank[5]]
        psX2 = bank[6]
        psG = bank[7]
        psC = bank[2]
        psH = [bank[2], bank[3]]
        psE = [bank[5], bank[6]]

        GROUPS = [(0, 4), (4, 10), (10, 16), (16, SLOT_TILES)]

        def group_of(s):
            return next(g for g, (a, b) in enumerate(GROUPS) if a <= s < b)

        block = ctx.enter_context(nc.Block())

        def tile_pipeline(stages):
            for k in range(SLOT_TILES + max(lag for lag, _ in stages)):
                for lag, do in sorted(stages, key=lambda s: -s[0]):
                    if 0 <= k - lag < SLOT_TILES:
                        do(k - lag)

        def pipeline(stages):
            last = NQ + max(lag for lag, _ in stages)
            for k in range(last):
                for lag, do in sorted(stages, key=lambda s: -s[0]):
                    if 0 <= k - lag < NQ:
                        do(k - lag)

        MV_ORDER = []
        pipeline([(lag, lambda q, n=n: MV_ORDER.append((n, q))) for n, lag in ((0, 0), (1, 6), (2, 7))])

        def mv_count(n, q):
            return MV_ORDER.index((n, q)) + 1

        RS_ORDER = []
        pipeline([(lag, lambda q, n=n: RS_ORDER.append((n, q))) for n, lag in ((0, 0), (1, 6), (2, 7))])

        def rs_count(n, q):
            return RS_ORDER.index((n, q)) + 1

        @block.sync
        def _(sp):
            for q in range(NQ):
                sp.dma_start(xin[:, q * TPC:(q + 1) * TPC, :],
                             xt_dram[:, q * TPC:(q + 1) * TPC, :]).then_inc(s_x[q], 16)
            sp.dma_start(w2_all[:], w2.rearrange("e (j p) d -> p (e j) d", p=P)).then_inc(s_w2, 16)
            sp.wait_ge(s_fill, 2)
            sp.wait_ge(s_norm, 32)
            sp.dma_start(s1_tiles, fill[:, None, 2 * C:].to_broadcast([P, SLOT_TILES, ROW1])).then_inc(s_filled1, 16)
            sp.dma_start(s2_tiles, fill[:, None, :].to_broadcast([P, SLOT_TILES, ROW2])).then_inc(s_filled2, 16)
            sp.wait_ge(s_sc1, 16 * NT)
            for g, (a, b) in enumerate(GROUPS):
                sp.dma_start(rows2[:, a:b, 2 * C:], s1_tiles[:, a:b, :]).then_inc(s_in2[g], 16)
            sp.wait_ge(s_sc2, 16 * SLOT_TILES)
            for g, (a, b) in enumerate(GROUPS):
                sp.dma_start(rows3[:, a:b, :], s2_tiles[:, a:b, :]).then_inc(s_in3[g], 16)
            sp.wait_ge(s_out, 16 * SLOT_TILES)

        @block.gpsimd
        def _(pool):
            g = nc.gpsimd
            g.memset(ident[:], 0.0).then_inc(s_const, 1)
            g.memset(before[:], 0.0).then_inc(s_const, 1)
            g.memset(minus_half[:], -0.5).then_inc(s_const, 1)
            pool.wait_ge(s_const, 2)
            g.affine_select(out=ident[:], in_=ident[:], compare_op=ALU.not_equal, fill=1.0, base=0,
                            pattern=[[-1, P]], channel_multiplier=1).then_inc(s_const, 1)
            g.affine_select(out=before[:], in_=before[:], compare_op=ALU.is_ge, fill=1.0, base=0,
                            pattern=[[-1, P]], channel_multiplier=1).then_inc(s_const, 1)
            g.memset(xnT[:, :, 0:1], 0.0).then_inc(s_const, 1)
            g.memset(sum_k[:, :, 0:1], 0.0).then_inc(s_const, 1)
            g.memset(sum_kv[:, :, 0:1], 0.0).then_inc(s_const, 1)
            g.memset(wk_eps[:], WK_EPS).then_inc(s_const, 1)
            g.memset(ln_eps[:], LN_EPS).then_inc(s_const, 1)
            g.memset(ones_b[:], 1.0).then_inc(s_const, 1)
            g.memset(ones_row[:], 1.0).then_inc(s_const, 1)
            g.memset(tile_keep[:], 1.0).then_inc(s_const, 1)
            g.memset(keep_e[:], 1.0).then_inc(s_const, 1)
            pool.wait_ge(s_const, 14)
            g.memset(tile_keep[:, :, :, 0:1], 0.0).then_inc(s_const, 1)
            g.memset(keep_e[:, :, 0:1], 0.0).then_inc(s_const, 1)
            g.iota(e_minus[:], pattern=[[1, E], [0, NT]], base=-E, channel_multiplier=0,
                   allow_small_or_imprecise_dtypes=True).then_inc(s_const, 1)
            g.iota(tile_start[:], pattern=[[0, 2 * E], [P, NT]], base=0, channel_multiplier=0,
                   allow_small_or_imprecise_dtypes=True).then_inc(s_const, 1)
            g.iota(slot_tile[:], pattern=[[0, 2], [1, SLOT_TILES], [0, E]], base=0, channel_multiplier=0,
                   allow_small_or_imprecise_dtypes=True).then_inc(s_const, 1)
            g.iota(rows1[:, :, C + A_TOK:C + A_TOK + 1].bitcast(I32), pattern=[[P, NT], [1, 1]], base=0,
                   channel_multiplier=1).then_inc(s_const, 1)
            g.memset(rows1[:, :, C + A_TOK + 1:], 0.0).then_inc(s_const, 1)
            g.memset(fill[:], 0.0).then_inc(s_fill, 1)
            pool.wait_ge(s_fill, 1)
            g.memset(fill[:, 2 * C + C + A_POS2:2 * C + C + A_TOK + 1].bitcast(I32), FILL).then_inc(s_fill, 1)

            def rstd(n, q):
                t = slice(q * TPC, (q + 1) * TPC)
                pool.wait_ge(s_mv, mv_count(n, q))
                g.tensor_scalar(veps[:, n, t], mv[:, n, t, 1], LN_EPS, None, ALU.add).then_inc(s_ve, 1)
                rstd.count += 1
                pool.wait_ge(s_ve, rstd.count)
                g.tensor_tensor(rs[:, n, t], veps[:, n, t], minus_half[:, t], ALU.pow).then_inc(s_rs, 1)

            rstd.count = 0

            def wk_sum(q):
                b, c, o = q // QPB, q % 2, (q % QPB) * CHUNK
                pool.wait_ge(s_uk, q + 1)
                pool.wait_ge(s_sk, q + 1)
                if q >= 2:
                    pool.wait_ge(s_rec, q - 1)
                g.tensor_tensor(wks[:, c], uk[:, c], sum_k[:, b, o:o + CHUNK], ALU.add).then_inc(s_wks, 1)
                pool.wait_ge(s_th, q + 1)
                g.tensor_scalar(sg[:, c], th[:, c], 0.5, 0.5, ALU.mult, ALU.add).then_inc(s_sg, 1)

            def rwkv(q):
                c = q % 2
                pool.wait_ge(s_wkv, q + 1)
                pool.wait_ge(s_rec, q + 1)
                g.tensor_tensor(yq[:, c], wkv[:, c], rec[:, c], ALU.mult).then_inc(s_yq, 1)
                pool.wait_ge(s_yq, q + 1)
                pool.wait_ge(s_sg, q + 1)
                if q >= 2:
                    pool.wait_ge(s_ops, q - 1)
                g.tensor_tensor(rw[:, c], yq[:, c], sg[:, c], ALU.mult).then_inc(s_rw, 1)

            pipeline([(0, lambda q: rstd(0, q)), (4, wk_sum), (5, rwkv),
                      (6, lambda q: rstd(1, q)), (7, lambda q: rstd(2, q))])

            pool.wait_ge(s_pos, 2)
            pool.wait_ge(s_filled1, 16)
            for i in range(NT):
                g.indirect_dma_start(sorted1, bass.IndirectOffsetOnAxis(ap=pos1[:, i:i + 1], axis=0),
                                     rows1[:, i, :], None).then_inc(s_sc1, 16)
            pool.wait_ge(s_filled2, 16)
            for s in range(SLOT_TILES):
                pool.wait_ge(s_row, s + 1)
                at = 3 * C + A_POS2
                g.indirect_dma_start(sorted2, bass.IndirectOffsetOnAxis(ap=rows2[:, s, at:at + 1].bitcast(I32), axis=0),
                                     rows2[:, s, :], None, bounds_check=SLOTS - 1, oob_is_err=False).then_inc(s_sc2, 16)
            for s in range(SLOT_TILES + 1):
                if s < SLOT_TILES:
                    pool.wait_ge(s_yy, s + 1)
                    g.tensor_tensor(rows3[:, s, C:2 * C], rows3[:, s, 0:C], rows3[:, s, 2 * C:3 * C],
                                    ALU.add).then_inc(s_fin, 1)
                if s >= 1:
                    pool.wait_ge(s_fin, s)
                    at = 3 * C + A_TOK
                    g.indirect_dma_start(out_rows, bass.IndirectOffsetOnAxis(ap=rows3[:, s - 1, at:at + 1].bitcast(I32), axis=0),
                                         rows3[:, s - 1, C:2 * C], None, bounds_check=TOKENS - 1,
                                         oob_is_err=False).then_inc(s_out, 16)

        @block.scalar
        def _(act):
            a = nc.scalar
            for n, w in enumerate((wk, wv, wr, wo)):
                act.dma_start(wnat[:, n, :], w).then_inc(s_wnat, 16)
            act.dma_start(mix[:], time_mix.rearrange("a b c -> c (a b)")).then_inc(s_small, 16)
            act.dma_start(decay_in[:], time_decay).then_inc(s_small, 16)
            act.dma_start(first_in[:], time_first).then_inc(s_small, 16)
            act.dma_start(gw[:], gate_w).then_inc(s_gate, 16)
            act.dma_start(gb[:], gate_b[None, :].to_broadcast([P, E])).then_inc(s_gate, 16)
            act.dma_start(w1_all[:, :, 0:H], w1.rearrange("e c h -> c e h")).then_inc(s_w1, 16)
            act.dma_start(b1_rows[:], b1.rearrange("e (j p) -> (e j) p", p=P)).then_inc(s_moe, 16)
            act.dma_start(b2_rows[:], b2.rearrange("(a e) d -> a (e d)", a=1).to_broadcast([3, E * C])).then_inc(s_b2, 16)
            act.dma_start(gamma[:], ln_gamma[None, :].to_broadcast([P, C])).then_inc(s_norm, 16)
            act.dma_start(beta[:], ln_beta[None, :].to_broadcast([P, C])).then_inc(s_norm, 16)
            act.wait_ge(s_small, 16 * 3)
            a.activation(decay_e[:], decay_in[:], ACT.Exp).then_inc(s_par, 1)
            act.wait_ge(s_par, 1)
            a.activation(decay[:], decay_e[:], ACT.Exp, scale=-1.0).then_inc(s_par, 1)
            a.activation(first[:], first_in[:], ACT.Exp).then_inc(s_par, 1)
            act.wait_ge(s_par, 3)
            act.wait_ge(s_const, CONSTS)
            act.wait_ge(s_wtps, 1)
            a.activation(wT[:].rearrange("p n c -> p (n c)"), bank[0][:], ACT.Copy).then_inc(s_wt, 1)
            act.wait_ge(s_b1ps, 1)
            a.activation(w1_all[:, :, H:], bank[1][:, 0:E * HC].rearrange("p (e j) -> p e j", j=HC),
                         ACT.Copy).then_inc(s_b1, 1)

            def xnt(q):
                b, c, o = q // QPB, q % 2, (q % QPB) * CHUNK
                act.wait_ge(s_xtps, q + 1)
                a.activation(xnT[:, b, 1 + o:1 + o + CHUNK], psX[:], ACT.Copy)
                if q >= 2:
                    act.wait_ge(s_xm, q - 1)
                a.activation(xmix[:, c], psX[:], ACT.Copy, scale=mix[:, 0:1]).then_inc(s_xt, 1)

            def kexp(q):
                c = q % 2
                act.wait_ge(s_kc, q + 1)
                if q >= 2:
                    act.wait_ge(s_kv, q - 1)
                    act.wait_ge(s_sk, q - 1)
                a.activation(ke[:, c], kc[:, c], ACT.Exp).then_inc(s_ke, 1)

            def sigmoid_uk(q):
                c = q % 2
                act.wait_ge(s_rps, q + 1)
                if q >= 2:
                    act.wait_ge(s_sg, q - 1)
                a.activation(th[:, c], psR[:], ACT.Tanh, scale=0.5).then_inc(s_th, 1)
                act.wait_ge(s_ke, q + 1)
                if q >= 2:
                    act.wait_ge(s_wks, q - 1)
                a.activation(uk[:, c], ke[:, c], ACT.Identity, bias=wk_eps[:, 0:1], scale=first[:, 0:1]).then_inc(s_uk, 1)

            def xn2t(q):
                act.wait_ge(s_x2ps, q + 1)
                if q >= 2:
                    act.wait_ge(s_gps, q - 1)
                a.activation(xn2T[:, q % 2], psX2[:], ACT.Copy).then_inc(s_x2t, 1)

            pipeline([(1, xnt), (3, kexp), (4, sigmoid_uk), (8, xn2t)])

            act.wait_ge(s_dl, 2)
            a.activation(el[:], dl[:], ACT.Exp).then_inc(s_el, 1)
            a.activation(e2[:], d2[:], ACT.Exp).then_inc(s_el, 1)

            def xT_copy(n):
                act.wait_ge(s_tps, n + 1)
                if n >= 2:
                    act.wait_ge(s_hps, n - 1)
                a.activation(xT[:, n % 2], psT[n % 2][:, 0:P], ACT.Copy).then_inc(s_tsb, 1)

            def relu(n):
                act.wait_ge(s_hps, n + 1)
                if n >= 3:
                    act.wait_ge(s_eps, n - 2)
                for j in range(HC):
                    ins = a.activation(hT[:, n % 3, j * P:(j + 1) * P], psH[n % 2][:, j * P:(j + 1) * P],
                                       ACT.Relu, bias=w1s[:, n % 4, H + j:H + j + 1])
                ins.then_inc(s_h, 1)

            def deviation(n, s):
                act.wait_ge(s_mv2[n], s + 1)
                a.activation(sd[:, n, s:s + 1], mv2[:, n, s, 1:2], ACT.Sqrt, bias=ln_eps[:, 0:1]).then_inc(s_sd[n], 1)

            def outer(s):
                act.wait_ge(s_shift, s + 1)
                a.activation(rows3[:, s, 0:C], rows3[:, s, C:2 * C], ACT.Identity, bias=shift[:, s:s + 1],
                             scale=rs2[:, 1, s:s + 1]).then_inc(s_yy, 1)

            tile_pipeline([(1, xT_copy), (2, relu)])
            tile_pipeline([(1, lambda s: xT_copy(SLOT_TILES + s)), (2, lambda s: relu(SLOT_TILES + s)),
                           (7, lambda s: deviation(0, s)), (11, lambda s: deviation(1, s)), (13, outer)])

        @block.tensor
        def _(pe):
            t = nc.tensor
            pe.wait_ge(s_const, CONSTS)
            pe.wait_ge(s_wnat, 64)
            for n in range(4):
                ins = t.transpose(bank[0][:, n * C:(n + 1) * C], wnat[:, n, :], ident[:])
            ins.then_inc(s_wtps, 1)
            pe.wait_ge(s_moe, 16)
            t.transpose(bank[1][:, 0:E * HC], b1_rows[:], ident[0:E * HC, 0:E * HC]).then_inc(s_b1ps, 1)

            def transpose_xn(q):
                pe.wait_ge(s_xn, q + 1)
                pe.wait_ge(s_wt, 1)
                if q >= 1:
                    pe.wait_ge(s_xt, q)
                for i in range(TPC):
                    ins = t.transpose(psX[:, i * P:(i + 1) * P], xn[:, q * TPC + i, :], ident[:])
                ins.then_inc(s_xtps, 1)

            def project_k(q):
                pe.wait_ge(s_xm, q + 1)
                if q >= 1:
                    pe.wait_ge(s_kc, q)
                t.matmul(psK[:], wT[:, 0, :], xm[:, q % 3], start=True, stop=True).then_inc(s_kps, 1)

            def project_vr(q):
                if q >= 1:
                    pe.wait_ge(s_kv, q)
                t.matmul(psV[:], wT[:, 1, :], xm[:, q % 3], start=True, stop=True).then_inc(s_vps, 1)
                if q >= 1:
                    pe.wait_ge(s_th, q)
                t.matmul(psR[:], wT[:, 2, :], xm[:, q % 3], start=True, stop=True).then_inc(s_rps, 1)

            def output(q):
                pe.wait_ge(s_rw, q + 1)
                if q >= 2:
                    pe.wait_ge(s_on, q - 1)
                if q == 0:
                    pe.wait_ge(s_b1, 1)
                for i in range(TPC):
                    ins = t.matmul(psO[q % 2][:, i * P:(i + 1) * P], rw[:, q % 2, i * P:(i + 1) * P], wT[:, 3, :],
                                   start=True, stop=True)
                ins.then_inc(s_ops, 1)

            def transpose_x2(q):
                pe.wait_ge(s_x2, q + 1)
                if q >= 1:
                    pe.wait_ge(s_x2t, q)
                for i in range(TPC):
                    ins = t.transpose(psX2[:, i * P:(i + 1) * P], xn[:, q * TPC + i, :], ident[:])
                ins.then_inc(s_x2ps, 1)

            def gate(q):
                pe.wait_ge(s_x2t, q + 1)
                if q == 0:
                    pe.wait_ge(s_gate, 32)
                for i in range(TPC):
                    n = q * TPC + i
                    ins = t.matmul(psG[:, n * E:(n + 1) * E], xn2T[:, q % 2, i * P:(i + 1) * P], gw[:],
                                   start=True, stop=True)
                ins.then_inc(s_gps, 1)

            pipeline([(1, transpose_xn), (3, project_k), (4, project_vr), (6, output), (8, transpose_x2), (9, gate)])

            pe.wait_ge(s_hot, 2)
            hots = hot[:].rearrange("p r e n -> p (r e n)")
            t.matmul(psC[:, 0:256], before[:], hots, start=True, stop=True)
            t.matmul(psC[:, 256:512], ones_b[:], hots, start=True, stop=True).then_inc(s_cnt, 1)

            def expert_of(r):
                return [pe.value_load(eid[0:1, r, s:s + 1], min_val=0, max_val=E - 1) for s in range(SLOT_TILES)]

            def turn(n):
                s = n % SLOT_TILES
                if n < SLOT_TILES:
                    pe.wait_ge(s_xs, n + 1)
                    src = rows2[:, s, C:2 * C]
                else:
                    pe.wait_ge(s_in3[group_of(s)], 16)
                    src = rows3[:, s, 0:C]
                if n >= 2:
                    pe.wait_ge(s_tsb, n - 1)
                t.transpose(psT[n % 2][:, 0:P], src, ident[:]).then_inc(s_tps, 1)

            def hidden(n):
                pe.wait_ge(s_tsb, n + 1)
                pe.wait_ge(s_w1s, n + 1)
                if n >= 2:
                    pe.wait_ge(s_h, n - 1)
                for j in range(HC):
                    ins = t.matmul(psH[n % 2][:, j * P:(j + 1) * P], w1s[:, n % 4, j * P:(j + 1) * P],
                                   xT[:, n % 2], start=True, stop=True)
                ins.then_inc(s_hps, 1)

            w2f = w2_all[:].rearrange("p a d -> p (a d)")

            def second(n, e):
                pe.wait_ge(s_h, n + 1)
                if 2 <= n < SLOT_TILES + 2:
                    pe.wait_ge(s_row, n - 1)
                elif n >= 2:
                    pe.wait_ge(s_res, n - 1 - SLOT_TILES)
                for j in range(HC):
                    t.matmul(psE[n % 2][:, 0:C], hT[:, n % 3, j * P:(j + 1) * P],
                             w2f[:, bass.ds(e * (HC * C) + j * C, C)], start=(j == 0), stop=False)
                t.matmul(psE[n % 2][:, 0:C], ones_row[:], b2_split[:, bass.ds(e * C, C)],
                         start=False, stop=True).then_inc(s_eps, 1)

            pe.wait_ge(s_eid, 1)
            pe.wait_ge(s_w2, 16)
            pe.wait_ge(s_b2s, 7)
            first_expert = expert_of(0)
            tile_pipeline([(1, turn), (2, hidden), (4, lambda s: second(s, first_expert[s]))])
            second_expert = expert_of(1)
            tile_pipeline([(1, lambda s: turn(SLOT_TILES + s)), (2, lambda s: hidden(SLOT_TILES + s)),
                           (4, lambda s: second(SLOT_TILES + s, second_expert[s]))])

        @block.vector
        def _(dve):
            v = nc.vector
            def moments(n, q, src):
                for i in range(TPC):
                    v_ = v.bn_stats(st[:, n, q * TPC + i, :], src(i))
                v_.then_inc(s_st, 1)
                moments.count += 1
                dve.wait_ge(s_st, moments.count)
                for i in range(TPC):
                    v_ = v.bn_aggr(mv[:, n, q * TPC + i, :], st[:, n, q * TPC + i, :])
                v_.then_inc(s_mv, 1)

            moments.count = 0

            def stats_x(q):
                dve.wait_ge(s_x[q], 16)
                moments(0, q, lambda i: xin[:, q * TPC + i, :])

            def norm_x(q):
                dve.wait_ge(s_rs, rs_count(0, q))
                for i in range(q * TPC, (q + 1) * TPC):
                    v_ = v.tensor_scalar(xn[:, i, :], xin[:, i, :], mv[:, 0, i, 0:1], rs[:, 0, i:i + 1],
                                         ALU.subtract, ALU.mult)
                v_.then_inc(s_xn, 1)

            def mix_x(q):
                b, c, o = q // QPB, q % 2, (q % QPB) * CHUNK
                dve.wait_ge(s_xt, q + 1)
                if q == 0:
                    dve.wait_ge(s_small, 16 * 3)
                    v.tensor_scalar(mix_rest[:], mix[:], -1.0, 1.0, ALU.mult, ALU.add).then_inc(s_rest, 1)
                    dve.wait_ge(s_rest, 1)
                    dve.wait_ge(s_par, 3)
                    dve.wait_ge(s_const, CONSTS)
                if q >= 3:
                    dve.wait_ge(s_rps, q - 2)
                v.scalar_tensor_tensor(xm[:, q % 3], xnT[:, b, o:o + CHUNK], mix_rest[:, 0:1], xmix[:, c],
                                       ALU.mult, ALU.add).then_inc(s_xm, 1)

            def clamp_k(q):
                dve.wait_ge(s_kps, q + 1)
                if q >= 2:
                    dve.wait_ge(s_ke, q - 1)
                v.tensor_scalar(kc[:, q % 2], psK[:], K_MAX, None, ALU.min).then_inc(s_kc, 1)

            def scans(q):
                b, c, o = q // QPB, q % 2, (q % QPB) * CHUNK
                dve.wait_ge(s_ke, q + 1)
                dve.wait_ge(s_vps, q + 1)
                v.tensor_tensor(kv[:, c], ke[:, c], psV[:], ALU.mult).then_inc(s_kv, 1)
                lam = decay[:, 0:1].to_broadcast([P, CHUNK])
                if q >= 1:
                    dve.wait_ge(s_skv, q)
                v.tensor_tensor_scan(sum_k[:, b, 1 + o:1 + o + CHUNK], lam, ke[:, c],
                                     sum_k[:, b, o:o + 1], ALU.mult, ALU.add).then_inc(s_sk, 1)
                dve.wait_ge(s_kv, q + 1)
                v.tensor_tensor_scan(sum_kv[:, b, 1 + o:1 + o + CHUNK], lam, kv[:, c],
                                     sum_kv[:, b, o:o + 1], ALU.mult, ALU.add).then_inc(s_skv, 1)

            def quotient(q):
                b, c, o = q // QPB, q % 2, (q % QPB) * CHUNK
                dve.wait_ge(s_skv, q + 1)
                if q >= 2:
                    dve.wait_ge(s_yq, q - 1)
                v.scalar_tensor_tensor(wkv[:, c], kv[:, c], first[:, 0:1], sum_kv[:, b, o:o + CHUNK],
                                       ALU.mult, ALU.add).then_inc(s_wkv, 1)
                dve.wait_ge(s_wks, q + 1)
                v.reciprocal(rec[:, c], wks[:, c]).then_inc(s_rec, 1)

            def stats_o(q):
                dve.wait_ge(s_ops, q + 1)
                moments(1, q, lambda i: psO[q % 2][:, i * P:(i + 1) * P])

            def residual(q):
                dve.wait_ge(s_rs, rs_count(1, q))
                for i in range(TPC):
                    n = q * TPC + i
                    v_ = v.tensor_scalar(on[:, q % 2, i, :], psO[q % 2][:, i * P:(i + 1) * P], mv[:, 1, n, 0:1],
                                         rs[:, 1, n:n + 1], ALU.subtract, ALU.mult)
                v_.then_inc(s_on, 1)
                dve.wait_ge(s_on, q + 1)
                v.tensor_tensor(rows1[:, q * TPC:(q + 1) * TPC, 0:C], on[:, q % 2],
                                xin[:, q * TPC:(q + 1) * TPC, :], ALU.add).then_inc(s_x1, 1)
                dve.wait_ge(s_x1, q + 1)
                moments(2, q, lambda i: rows1[:, q * TPC + i, 0:C])

            def norm_x1(q):
                dve.wait_ge(s_rs, rs_count(2, q))
                dve.wait_ge(s_xtps, q + 1)
                for i in range(q * TPC, (q + 1) * TPC):
                    v_ = v.tensor_scalar(xn[:, i, :], rows1[:, i, 0:C], mv[:, 2, i, 0:1], rs[:, 2, i:i + 1],
                                         ALU.subtract, ALU.mult)
                v_.then_inc(s_x2, 1)

            pipeline([(0, stats_x), (1, norm_x), (2, mix_x), (3, clamp_k), (4, scans),
                      (5, quotient), (6, stats_o), (7, residual), (8, norm_x1)])

            def by_tile(ap):
                return ap.rearrange("p e n -> p n e")

            def per_expert(ap):
                return ap[:, None, :].to_broadcast([P, E, NT])

            count = [0]

            def step(ins):
                ins.then_inc(s_r, 1)
                count[0] += 1
                dve.wait_ge(s_r, count[0])

            dve.wait_ge(s_gps, NQ)
            dve.wait_ge(s_gate, 32)
            step(v.tensor_tensor(logit[:], psG[:, 0:NT * E].rearrange("p (n e) -> p e n", e=E),
                                 gb[:, :, None].to_broadcast([P, E, NT]), ALU.add))
            for r, src in ((0, logit), (1, rest)):
                step(v.tensor_reduce(top[:, r, :], by_tile(src[:]), AXX, ALU.max))
                step(v.tensor_tensor(same[:], src[:], per_expert(top[:, r, :]), ALU.is_equal))
                step(v.tensor_tensor(key[:], same[:], e_minus[:], ALU.mult))
                step(v.tensor_reduce(pick[:, r, :], by_tile(key[:]), AXX, ALU.min))
                ins = v.tensor_tensor(hot[:, r], e_minus[:], per_expert(pick[:, r, :]), ALU.is_equal)
                ins.then_inc(s_hot, 1)
                dve.wait_ge(s_hot, r + 1)
                if r == 0:
                    step(v.scalar_tensor_tensor(rest[:], hot[:, 0], -BIG, logit[:], ALU.mult, ALU.add))
            v.tensor_tensor(dl[:], logit[:], per_expert(top[:, 0, :]), ALU.subtract).then_inc(s_dl, 1)
            v.tensor_tensor(d2[:], top[:, 1, :], top[:, 0, :], ALU.subtract).then_inc(s_dl, 1)

            dve.wait_ge(s_cnt, 1)
            totals = psC[:, 256:512]
            flat = lambda ap: ap.rearrange("p r e n -> p (r e n)")
            step(v.tensor_tensor_scan(flat(upto[:]), flat(tile_keep[:]), totals, 0.0, ALU.mult, ALU.add))
            counts = upto[:, :, :, NT - 1:NT].to_broadcast([P, 2, E, NT])
            v.tensor_tensor(flat(less[:]), flat(upto[:]), totals, ALU.subtract).then_inc(s_r, 1)
            count[0] += 1
            step(v.tensor_tensor(longer[:], counts, tile_start[:], ALU.is_gt))
            step(v.tensor_reduce(ntile[:], longer[:], AXX, ALU.add))
            step(v.tensor_tensor_scan(cum[:].rearrange("p r e -> p (r e)"), keep_e[:].rearrange("p r e -> p (r e)"),
                                      ntile[:].rearrange("p r e -> p (r e)"), 0.0, ALU.mult, ALU.add))
            step(v.tensor_tensor(base[:], cum[:], ntile[:], ALU.subtract))
            step(v.tensor_tensor(flat(place[:]), flat(less[:]), psC[:, 0:256], ALU.add))
            step(v.scalar_tensor_tensor(less[:].rearrange("p r e n -> p (r e) n"),
                                        base[:].rearrange("p r e -> p (r e)")[:, :, None].to_broadcast([P, 2 * E, NT]),
                                        float(P), place[:].rearrange("p r e n -> p (r e) n"), ALU.mult, ALU.add))
            step(v.tensor_tensor(place[:], less[:], hot[:], ALU.mult))
            with nc.allow_low_precision(reason="slots are whole numbers far below 2 ** 24"):
                v.tensor_reduce(pos1[:], by_tile(place[:, 0]), AXX, ALU.add).then_inc(s_r, 1)
                v.tensor_reduce(rows1[:, :, C + A_POS2].bitcast(I32), by_tile(place[:, 1]), AXX,
                                ALU.add).then_inc(s_r, 1)
            count[0] += 2
            dve.wait_ge(s_el, 2)
            step(v.tensor_reduce(den[:], by_tile(el[:]), AXX, ALU.add))
            step(v.reciprocal(rows1[:, :, C + A_G0], den[:]))
            v.tensor_tensor(rows1[:, :, C + A_G1], e2[:], rows1[:, :, C + A_G0], ALU.mult)
            v.tensor_copy(rows1[:, :, C + A_MEAN], mv[:, 2, :, 0])
            v.tensor_copy(rows1[:, :, C + A_RSTD], rs[:, 2, :]).then_inc(s_pos, 2)
            step(v.tensor_tensor(done_e[:], cum[0:1, :, None, :].to_broadcast([1, 2, SLOT_TILES, E]),
                                 slot_tile[:], ALU.is_le))
            step(v.tensor_reduce(eid_f[:], done_e[:], AXX, ALU.add))
            v.tensor_scalar(eid[:], eid_f[:], float(E - 1), None, ALU.min).then_inc(s_eid, 1)
            dve.wait_ge(s_eid, 1)

            dve.wait_ge(s_b2, 16)
            dve.wait_ge(s_const, CONSTS)
            is_part = [ident[0:3, i:i + 1] for i in range(3)]
            v.tensor_copy(b2_part[:, 0], b2_rows[:]).then_inc(s_b2s, 1)
            dve.wait_ge(s_b2s, 1)
            v.tensor_scalar(b2_split[:], b2_part[:, 0], is_part[0], None, ALU.mult).then_inc(s_b2s, 1)
            v.tensor_tensor(b2_rows[:], b2_rows[:], b2_part[:, 0], ALU.subtract).then_inc(s_b2s, 1)
            dve.wait_ge(s_b2s, 3)
            v.tensor_copy(b2_part[:, 1], b2_rows[:]).then_inc(s_b2s, 1)
            dve.wait_ge(s_b2s, 4)
            v.scalar_tensor_tensor(b2_split[:], b2_part[:, 1], is_part[1], b2_split[:], ALU.mult, ALU.add).then_inc(s_b2s, 1)
            v.tensor_tensor(b2_rows[:], b2_rows[:], b2_part[:, 1], ALU.subtract).then_inc(s_b2s, 1)
            dve.wait_ge(s_b2s, 6)
            v.scalar_tensor_tensor(b2_split[:], b2_rows[:], is_part[2], b2_split[:], ALU.mult, ALU.add).then_inc(s_b2s, 1)

            w1f = w1_all[:].rearrange("p e h -> p (e h)")

            def expert_of(r):
                return [dve.value_load(eid[0:1, r, s:s + 1], min_val=0, max_val=E - 1) for s in range(SLOT_TILES)]

            def stage_w1(n, e):
                if n >= 4:
                    dve.wait_ge(s_h, n - 3)
                v.tensor_copy(w1s[:, n % 4, :], w1f[:, bass.ds(e * (H + HC), H + HC)]).then_inc(s_w1s, 1)

            def aux(rows, s, what):
                return rows[:, s, 3 * C + what:3 * C + what + 1]

            def norm_rows(s):
                dve.wait_ge(s_in2[group_of(s)], 16)
                v.tensor_scalar(rows2[:, s, C:2 * C], rows2[:, s, 2 * C:3 * C], aux(rows2, s, A_MEAN),
                                aux(rows2, s, A_RSTD), ALU.subtract, ALU.mult).then_inc(s_xs, 1)

            def write_row(s):
                dve.wait_ge(s_eps, s + 1)
                v.scalar_tensor_tensor(rows2[:, s, 0:C], psE[s % 2][:, 0:C], ALPHA, rows2[:, s, C:2 * C],
                                       ALU.mult, ALU.add)
                v.scalar_tensor_tensor(rows2[:, s, C:2 * C], psE[s % 2][:, 0:C], aux(rows2, s, A_G0),
                                       rows2[:, s, C:2 * C], ALU.mult, ALU.add).then_inc(s_row, 1)

            dve.wait_ge(s_w1, 16)
            dve.wait_ge(s_b1, 1)
            first_expert = expert_of(0)
            tile_pipeline([(0, lambda s: stage_w1(s, first_expert[s])), (0, norm_rows), (5, write_row)])

            low, mid = (lambda s: rows3[:, s, 0:C]), (lambda s: rows3[:, s, C:2 * C])

            def add_choice(s):
                n = SLOT_TILES + s
                dve.wait_ge(s_eps, n + 1)
                dve.wait_ge(s_in3[group_of(s)], 16)
                v.scalar_tensor_tensor(mid(s), psE[n % 2][:, 0:C], aux(rows3, s, A_G1), mid(s),
                                       ALU.mult, ALU.add).then_inc(s_res, 1)

            def stats2(n, s):
                dve.wait_ge((s_res, s_zz)[n], s + 1)
                v.bn_stats(st2[:, n, s, :], mid(s)).then_inc(s_st2[n], 1)

            def moments2(n, s):
                dve.wait_ge(s_st2[n], s + 1)
                v.bn_aggr(mv2[:, n, s, :], st2[:, n, s, :]).then_inc(s_mv2[n], 1)

            def times_gamma(s):
                dve.wait_ge(s_mv2[0], s + 1)
                dve.wait_ge(s_tps, SLOT_TILES + s + 1)
                v.scalar_tensor_tensor(low(s), mid(s), mv2[:, 0, s, 0:1], gamma[:], ALU.subtract,
                                       ALU.mult).then_inc(s_tg, 1)

            def rstd2(n, s):
                dve.wait_ge(s_sd[n], s + 1)
                v.reciprocal(rs2[:, n, s:s + 1], sd[:, n, s:s + 1]).then_inc(s_rs2[n], 1)

            def inner(s):
                dve.wait_ge(s_tg, s + 1)
                dve.wait_ge(s_rs2[0], s + 1)
                v.scalar_tensor_tensor(mid(s), low(s), rs2[:, 0, s:s + 1], beta[:], ALU.mult,
                                       ALU.add).then_inc(s_zz, 1)

            def outer_shift(s):
                dve.wait_ge(s_rs2[1], s + 1)
                v.scalar_tensor_tensor(shift[:, s:s + 1], mv2[:, 1, s, 0:1], -1.0, rs2[:, 1, s:s + 1],
                                       ALU.mult, ALU.mult).then_inc(s_shift, 1)

            dve.wait_ge(s_norm, 32)
            second_expert = expert_of(1)
            tile_pipeline([(0, lambda s: stage_w1(SLOT_TILES + s, second_expert[s])), (5, add_choice),
                           (6, lambda s: stats2(0, s)), (7, lambda s: moments2(0, s)),
                           (8, times_gamma), (8, lambda s: rstd2(0, s)), (9, inner),
                           (10, lambda s: stats2(1, s)), (11, lambda s: moments2(1, s)),
                           (12, lambda s: rstd2(1, s)), (13, outer_shift)])


_INS = ['L0_attn_x', 'L0_attn_time_decay', 'L0_attn_time_first', 'L0_attn_time_mix', 'L0_attn_Wk',
        'L0_attn_Wv', 'L0_attn_Wr', 'L0_attn_Wo', 'L0_ffn_gate_W', 'L0_ffn_gate_b', 'L0_ffn_W1',
        'L0_ffn_b1', 'L0_ffn_W2', 'L0_ffn_b2', 'L0_ffn_ln_gamma', 'L0_ffn_ln_beta']


def kernel(**inputs):
    import numpy as np
    import concourse.bacc as bacc
    from concourse.bass_utils import run_bass_kernel_spmd as run

    nc = bacc.Bacc("TRN2", target_bir_lowering=False, num_devices=1)
    arrays, args = {}, []
    for name in _INS:
        a = np.ascontiguousarray(inputs[name])
        arrays[f"in_{name}"] = a
        args.append(nc.dram_tensor(f"in_{name}", a.shape, mybir.dt.from_np(a.dtype), kind="ExternalInput").ap())
    o = nc.dram_tensor("o", arrays["in_L0_attn_x"].shape, F32, kind="ExternalOutput").ap()
    build_program(nc, *args, o)
    r = run(nc, [arrays], core_ids=[0])
    return r.results[0]["o"]
```

```python
import math
from contextlib import ExitStack

import concourse.bass as bass
from concourse import mybir

ALU = mybir.AluOpType
ACT = mybir.ActivationFunctionType
AXX = mybir.AxisListType.X
F32 = mybir.dt.float32
BF16 = mybir.dt.bfloat16
I32 = mybir.dt.int32

P = 128
LN_EPS = 1e-5
K_MAX = 60.0
EXP_MAX = math.exp(K_MAX)
WK_EPS = 1e-9
ALPHA = 0.5
CHUNK = 512
TPC = CHUNK // P
LAG = dict(
    stats_x=0.41, shift_x=0.49, mix_x=3.07, kv_scans=4.32, quotient=5.22,
    stats_o=6.98, residual=7.53, stats_x1=8.14, scale_logits=8.64, add_gate_bias=8.92,
    sort_logits=9.06, sort_experts=9.08, gate_shift=9.09, onehots=9.1, place=9.4,
    gates=9.52,
    rstd_x=-1.65, clamp_k=8.62, wk_sum=9.51, rwkv=10.39, gated=10.62,
    rstd_o=11.74, rstd_x1=13.09, scatter_0=14.8, scatter_1=14.26,
    scatter_2=14.62, scatter_3=14.37,
    transpose_xn=0.3, project_k=1.42, project_vr=1.96, output=4.87, transpose_x1=6.43,
    gate=7.12, places=7.75,
    norm_x=-0.56, copy_xn=0.1, exp_k=1.32, tanh_uk=1.65, copy_x1=7.19, gate_exp=7.71)
AUX = 8
A_MEAN, A_VAR, A_RSTD, A_G0, A_G1, A_POS1, A_POS2, A_TOK = range(AUX)


def build_program(nc, x, time_decay, time_first, time_mix, wk, wv, wr, wo,
                  gate_w, gate_b, w1, b1, w2, b2, ln_gamma, ln_beta, out):
    B, T, C = x.shape
    E, _, H = w1.shape
    TOKENS = B * T
    NT = TOKENS // P
    NQ = TOKENS // CHUNK
    QPB = T // CHUNK
    HC = H // P
    SLOT_TILES = NT + E - 1
    BIN_TILES = NT + 1
    BIN = BIN_TILES * P
    NO_TILE = E * BIN_TILES
    SLOTS = (NO_TILE + 1) * P
    ROW1 = C + AUX
    ROW2 = C + ROW1
    STAGED = 6
    ROWS_AHEAD = 5
    FILL = 1 << 20
    assert C == P and T % CHUNK == 0 and H == HC * P

    xt_dram = x.rearrange("b t c -> (b t) c").rearrange("(n p) c -> p n c", p=P)
    out_rows = out.rearrange("b t c -> (b t) c")
    out_tiles = out_rows.rearrange("(n p) c -> p n c", p=P)
    sorted1 = nc.dram_tensor("sorted1", (SLOTS, ROW1), F32, kind="Internal").ap()
    sorted2 = nc.dram_tensor("sorted2", (SLOTS, ROW2), F32, kind="Internal").ap()

    with ExitStack() as ctx:
        def sb(name, shape, dt=F32):
            return ctx.enter_context(nc.sbuf_tensor(name, shape, dt))

        def sem(name):
            return ctx.enter_context(nc.semaphore(name))

        bank = [ctx.enter_context(nc.psum_tensor(f"bank{i}", [P, 512], F32)) for i in range(8)]

        wnat = sb("wnat", [P, 4, C])
        wT = sb("wT", [P, 4, C])
        decay_in = sb("decay_in", [P, 1])
        first_in = sb("first_in", [P, 1])
        mix = sb("mix", [P, 1])
        mix_rest = sb("mix_rest", [P, 1])
        decay_e = sb("decay_e", [P, 1])
        decay = sb("decay", [P, 1])
        first = sb("first", [P, 1])
        wk_eps = sb("wk_eps", [P, 1])
        gw = sb("gw", [P, E])
        gwc = sb("gwc", [P, E])
        wo_sum = sb("wo_sum", [P, 1])
        wo_mean = sb("wo_mean", [P, 1])
        gb = sb("gb", [P, E])
        w1_all = sb("w1_all", [P, E, H + HC])
        b1_rows = sb("b1_rows", [E * HC, P])
        w2_all = sb("w2_all", [P, E * HC, C])
        b2_rows = sb("b2_rows", [E, C])
        b2_part = sb("b2_part", [E, 3, C], BF16)
        b2_split = sb("b2_split", [3, E * C], BF16)
        gamma = sb("gamma", [P, C])
        beta = sb("beta", [P, C])
        ident = sb("ident", [P, P])
        before = sb("before", [P, P], BF16)
        ones_b = sb("ones_b", [P, P], BF16)
        spin = sb("spin", [P, 512], BF16)
        ones_row = sb("ones_row", [3, P], BF16)
        minus_half = sb("minus_half", [P, NT])
        all_ones = sb("all_ones", [P, P])
        expert_no = sb("expert_no", [P, E])
        bin_start = sb("bin_start", [1, TPC, 2, E], BF16)
        slot_tile = sb("slot_tile", [1, SLOT_TILES, E])
        keep_e = sb("keep_e", [1, E])
        fill = sb("fill", [P, ROW2])

        rows2 = sb("rows2", [P, SLOT_TILES, ROW2])
        rows3 = sb("rows3", [P, SLOT_TILES, ROW2])
        taken = {"rows2": 0, "rows3": 0}

        def over(name, a, b):
            at = taken[name]
            taken[name] += a * b
            assert taken[name] <= SLOT_TILES * ROW2
            flat_rows = (rows2 if name == "rows2" else rows3)[:].rearrange("p s w -> p (s w)")
            return flat_rows[:, at:at + a * b].rearrange("p (a b) -> p a b", b=b)

        xin = sb("xin", [P, NT, C])
        st = sb("st", [P, 3, NT, 6])
        mv = sb("mv", [P, 3, NT, 2])
        veps = sb("veps", [P, 3, NT])
        shift_in = sb("shift_in", [P, NT])
        rs = sb("rs", [P, 3, NT])
        xn = sb("xn", [P, NT, C])
        xnT = over("rows3", B, T + 1)
        xmix = over("rows3", 2, CHUNK)
        xm = over("rows3", 3, CHUNK)
        exp_k = sb("exp_k", [P, 2, CHUNK])
        ke = over("rows2", 2, CHUNK)
        kv = over("rows3", 2, CHUNK)
        th = sb("th", [P, 2, CHUNK])
        uk = over("rows2", 2, CHUNK)
        sg = over("rows2", 2, CHUNK)
        sum_k = sb("sum_k", [P, B, T + 1])
        sum_kv = sb("sum_kv", [P, B, T + 1])
        wkv = sb("wkv", [P, 2, CHUNK])
        wks = over("rows2", 2, CHUNK)
        rec = over("rows2", 2, CHUNK)
        yq = sb("yq", [P, 2, CHUNK])
        rw = sb("rw", [P, 2, CHUNK])
        on = sb("on", [P, 2, TPC, C])
        rows1 = sb("rows1", [P, NT, ROW1])
        x1T = sb("x1T", [P, 2, CHUNK])

        scaled = sb("scaled", [P, NT, E])
        logit = sb("logit", [P, NT, E])
        top = sb("top", [P, NT, E])
        topi = sb("topi", [P, NT, E], mybir.dt.uint32)
        hot = sb("hot", [P, NT, 2, E], BF16)
        dl = sb("dl", [P, NT, E])
        el = sb("el", [P, NT, E])
        den = sb("den", [P, NT])
        placed = sb("placed", [P, NT, 2, E])
        count_i = sb("count_i", [1, 2, E], I32)
        count_up = sb("count_up", [1, 2, E], I32)
        ntile_i = sb("ntile_i", [1, 2, E], I32)
        cum = sb("cum", [1, 2, E])
        skip = sb("skip", [1, 2, E])
        done_e = sb("done_e", [1, 2, SLOT_TILES, E])
        skipped = sb("skipped", [1, 2, SLOT_TILES, E])
        eid_f = sb("eid_f", [1, 2, SLOT_TILES])
        tid_f = sb("tid_f", [1, 2, SLOT_TILES])
        tid_s = sb("tid_s", [1, 2, SLOT_TILES])
        eid = sb("eid", [1, 2, SLOT_TILES], I32)
        tid = sb("tid", [1, 2, SLOT_TILES], I32)

        w1s = sb("w1s", [P, STAGED, H + HC])
        xT = sb("xT", [P, 2, P])
        hT = sb("hT", [P, 3, H])
        st2 = sb("st2", [P, 2, SLOT_TILES, 6])
        mv2 = sb("mv2", [P, 2, SLOT_TILES, 2])
        sd = sb("sd", [P, 2, SLOT_TILES])
        rs2 = sb("rs2", [P, 2, SLOT_TILES])
        shift = sb("shift", [P, SLOT_TILES])
        ln_eps = sb("ln_eps", [P, 1])

        s_w1d = sem("w1_staged")
        s_w1s = [sem(f"w1_staged{i}") for i in range(STAGED)]
        LOADS = 8
        CONSTS = 19
        s_x = [sem(f"x_in{q}") for q in range(NQ)]
        s_wnat = sem("wnat_in")
        s_small = sem("small_in")
        s_gate = sem("gate_in")
        s_w1 = sem("w1_in")
        s_w2 = sem("w2_in")
        s_moe = sem("b1_in")
        s_b2 = sem("b2_in")
        s_b2s = sem("b2_parts")
        s_b2r = sem("b2_part_rows")
        s_ident = sem("identity")
        s_norm = sem("norm_in")
        s_const = sem("consts")
        s_fill = sem("fill_ready")
        s_filled = [sem("sorted1_filled"), sem("sorted2_filled")]
        s_wtps = sem("wT_psum")
        s_wt = sem("wT_ready")
        s_b1ps = sem("b1_psum")
        s_b1 = sem("b1_ready")
        s_par = sem("params")
        s_rest = sem("mix_rest_ready")
        s_st = [sem(f"stats_{n}") for n in ("x", "o", "x1")]
        s_mv = [sem(f"moments_{n}") for n in ("x", "o", "x1")]
        s_ve = [sem(f"var_eps_{n}") for n in ("x", "o", "x1")]
        s_rs = [sem(f"rstd_{n}") for n in ("x", "o", "x1")]
        s_shx = sem("x_shift")
        s_xn = sem("xn")
        s_xtps = sem("xnT_psum")
        s_xt = sem("xnT")
        s_xm = sem("xm")
        s_kps = sem("k_psum")
        s_vps = sem("v_psum")
        s_rps = sem("r_psum")
        s_kc = sem("exp_k_bounded")
        s_ke = sem("exp_k")
        s_th = sem("tanh")
        s_uk = sem("uk")
        s_kv = sem("kv")
        s_sk = sem("scan_k")
        s_skv = sem("scan_kv")
        s_wkv = sem("wkv")
        s_wks = sem("wk_sum")
        s_rec = sem("recip")
        s_sg = sem("sigmoid")
        s_yq = sem("quotient")
        s_rw = sem("rwkv")
        s_ops = sem("o_psum")
        s_x1 = sem("x1")
        s_x1ps = sem("x1T_psum")
        s_x1t = sem("x1T")
        s_gsum = sem("gate_weight_sums")
        s_gwc = sem("gate_weights_centered")
        s_wo = sem("wo_centering")
        s_sc = sem("logits_scaled")
        s_lo = sem("logits")
        s_top = sem("logits_sorted")
        s_topi = sem("experts_sorted")
        s_bins = sem("bin_counts_psum")
        s_placed = sem("placed")
        s_den = sem("gate_sums")
        s_g0 = sem("first_gates")
        s_gates = sem("gates")
        s_gps = sem("gate_psum")
        s_hot = sem("onehots")
        s_cnt = sem("counts_psum")
        s_dl = sem("gate_shifted")
        s_el = sem("gate_exp")
        s_pos = sem("positions")
        s_cn = sem("counts")
        s_tr = sem("tile_route_steps")
        s_eid = sem("expert_ids")
        s_sc1 = sem("scatter1")
        s_in2 = [sem(f"rows2_in{i}") for i in range(LOADS)]
        s_sc2 = sem("scatter2")
        s_in3 = [sem(f"rows3_in{i}") for i in range(LOADS)]
        s_out_x1 = sem("out_holds_x1")
        s_out = sem("out_rows")
        s_xs = sem("xs")
        s_tps = sem("xsT_psum")
        s_tsb = sem("xsT")
        s_hps = sem("h_psum")
        s_h = sem("h")
        s_eps = sem("expert_psum")
        s_row = sem("row2_written")
        s_res = sem("residual_sum")
        s_st2 = [sem("inner_stats"), sem("outer_stats")]
        s_mv2 = [sem("inner_moments"), sem("outer_moments")]
        s_sd = [sem("inner_deviation"), sem("outer_deviation")]
        s_rs2 = [sem("inner_rstd"), sem("outer_rstd")]
        s_tg = sem("times_gamma")
        s_zz = sem("inner_norm")
        s_shift = sem("outer_shift")
        s_yy = sem("outer_norm")

        psX = bank[0][:, 0:CHUNK]
        psT = [bank[0], bank[1]]
        psK, psV, psR = (bank[i][:, 0:CHUNK] for i in (2, 3, 4))
        psO = [bank[5], bank[1]]
        psX1 = bank[6][:, 0:CHUNK]
        psG = bank[7][:, 0:NT * E]
        psP = bank[7][:, NT * E:NT * E + NT * 2 * E]
        psN = bank[2][:, 0:2 * E]
        psH = [bank[2], bank[3]]
        psE = [bank[5], bank[6]]

        block = ctx.enter_context(nc.Block())

        def pair(s):
            if s % 2 == 1:
                return slice(s - 1, s + 1)
            return slice(s, s + 1) if s == SLOT_TILES - 1 else None

        def pairs(s):
            return s // 2 + 1

        def tile_pipeline(stages):
            todo = [(s + lag, -lag, n, s, do) for n, (lag, do) in enumerate(stages) for s in range(SLOT_TILES)]
            for *_, s, do in sorted(todo, key=lambda t: t[:3]):
                do(s)

        def tiles_of(q):
            return slice(q * TPC, (q + 1) * TPC)

        def pipeline(stages):
            todo = [(q + LAG[name], q, do) for name, do in stages.items() for q in range(NQ)]
            for _, q, do in sorted(todo, key=lambda t: t[:2]):
                do(q)

        @block.sync
        def _(sp):
            def load_x(q):
                sp.dma_start(xin[:, q * TPC:(q + 1) * TPC, :],
                             xt_dram[:, q * TPC:(q + 1) * TPC, :]).then_inc(s_x[q], 16)

            load_x(0)
            sp.dma_start(wnat[:, 1, :], wv).then_inc(s_wnat, 16)
            sp.dma_start(wnat[:, 3, :], wo).then_inc(s_wnat, 16)
            load_x(1)
            sp.dma_start(gw[:], gate_w).then_inc(s_gate, 16)
            sp.dma_start(gb[:], gate_b[None, :].to_broadcast([P, E])).then_inc(s_gate, 16)
            sp.dma_start(b2_rows[:], b2).then_inc(s_b2, 16)
            for q in range(2, NQ):
                load_x(q)
            sp.dma_start(b1_rows[:], b1.rearrange("e (j p) -> (e j) p", p=P)).then_inc(s_moe, 16)
            sp.dma_start(w1_all[:, :, 0:H], w1.rearrange("e c h -> c e h")).then_inc(s_w1, 16)
            sp.dma_start(w2_all[:], w2.rearrange("e (j p) d -> p (e j) d", p=P)).then_inc(s_w2, 16)
            sp.dma_start(gamma[:], ln_gamma[None, :].to_broadcast([P, C])).then_inc(s_norm, 16)
            sp.dma_start(beta[:], ln_beta[None, :].to_broadcast([P, C])).then_inc(s_norm, 16)
            for q in range(NQ):
                sp.wait_ge(s_x1, q + 1)
                sp.dma_start(out_tiles[:, q * TPC:(q + 1) * TPC, :],
                             rows1[:, q * TPC:(q + 1) * TPC, 0:C]).then_inc(s_out_x1, 16)
            sp.wait_ge(s_b2s, 5)
            for i in range(3):
                sp.dma_start(b2_split[i:i + 1, :].rearrange("a (e d) -> a e d", e=E), b2_part[:, i, :]).then_inc(s_b2r, 16)
            sp.wait_ge(s_fill, 2)
            filler = (fill[:, C:], fill[:])
            sorted_rows = (sorted1, sorted2)
            for r in range(2):
                sp.dma_start(sorted_rows[r][NO_TILE * P:, :], filler[r]).then_inc(s_filled[r], 16)

            def values(ap, high):
                return nc.values_load_multi_w_load_instructions(
                    ap, engines=[mybir.EngineType.SP], min_val=0, max_val=high,
                    skip_runtime_bounds_check_because="counts of tokens and of tiles, cut off on the chip")[1]

            def fill_tails(r):
                n = values(count_i[0:1, r, :], TOKENS)
                for e in range(E):
                    sp.dma_start(sorted_rows[r][bass.ds(n[e] + e * BIN, P), :], filler[r]).then_inc(s_filled[r], 16)

            w1f = w1_all[:].rearrange("p e h -> p (e h)")

            def stage_w1(s, e):
                n = SLOT_TILES + s
                sp.wait_ge(s_h, n - STAGED + 1)
                sp.dma_start(w1s[:, n % STAGED, :], w1f[:, bass.ds(e * (H + HC), H + HC)]).then_inc(s_w1s[n % STAGED], 16)

            def load_row(r, s, tile, dst, s_in):
                if s >= LOADS:
                    sp.wait_ge(s_in[s % LOADS], 16 * (s // LOADS))
                if s == 0:
                    sp.wait_ge(s_filled[r], 16 * (E + 1))
                    sp.wait_ge((s_sc1, s_sc2)[r], 16 * (NT, SLOT_TILES)[r])
                sp.dma_start(dst, sorted_rows[r][bass.ds(tile * P, P), :]).then_inc(s_in[s % LOADS], 16)

            sp.wait_ge(s_cn, 1)
            fill_tails(0)
            sp.wait_ge(s_eid, 1)
            tile = values(tid[0:1, 0, :], NO_TILE)
            for s in range(SLOT_TILES):
                load_row(0, s, tile[s], rows2[:, s, C:], s_in2)
            fill_tails(1)
            sp.wait_ge(s_eid, 2)
            tile = values(tid[0:1, 1, :], NO_TILE)
            expert = values(eid[0:1, 1, :], E - 1)
            for s in range(STAGED):
                stage_w1(s, expert[s])
            for s in range(SLOT_TILES + ROWS_AHEAD):
                if s < SLOT_TILES:
                    load_row(1, s, tile[s], rows3[:, s, :], s_in3)
                if ROWS_AHEAD <= s < SLOT_TILES - STAGED + ROWS_AHEAD:
                    stage_w1(s - ROWS_AHEAD + STAGED, expert[s - ROWS_AHEAD + STAGED])
            sp.wait_ge(s_out, 16 * SLOT_TILES)

        @block.gpsimd
        def _(pool):
            g = nc.gpsimd
            g.memset(ident[:], 0.0).then_inc(s_const, 1)
            g.memset(before[:], 0.0).then_inc(s_const, 1)
            g.memset(minus_half[:], -0.5).then_inc(s_const, 1)
            pool.wait_ge(s_const, 2)
            g.affine_select(out=ident[:], in_=ident[:], compare_op=ALU.not_equal, fill=1.0, base=0,
                            pattern=[[-1, P]], channel_multiplier=1).then_inc(s_ident, 1)
            g.affine_select(out=before[:], in_=before[:], compare_op=ALU.is_ge, fill=1.0, base=0,
                            pattern=[[-1, P]], channel_multiplier=1).then_inc(s_const, 1)
            g.memset(xnT[:, :, 0:1], 0.0).then_inc(s_const, 1)
            g.memset(sum_k[:, :, 0:1], 0.0).then_inc(s_const, 1)
            g.memset(sum_kv[:, :, 0:1], 0.0).then_inc(s_const, 1)
            g.memset(wk_eps[:], WK_EPS).then_inc(s_const, 1)
            g.memset(ln_eps[:], LN_EPS).then_inc(s_const, 1)
            g.memset(ones_b[:], 1.0).then_inc(s_const, 1)
            g.memset(ones_row[:], 1.0).then_inc(s_const, 1)
            g.memset(spin[:], 1.0).then_inc(s_const, 1)
            g.memset(all_ones[:], 1.0).then_inc(s_const, 1)
            g.memset(keep_e[:], 1.0).then_inc(s_const, 1)
            pool.wait_ge(s_const, 14)
            g.memset(keep_e[:, 0:1], 0.0).then_inc(s_const, 1)
            g.iota(expert_no[:], pattern=[[1, E]], base=0, channel_multiplier=0,
                   allow_small_or_imprecise_dtypes=True).then_inc(s_const, 1)
            g.iota(bin_start[:], pattern=[[0, TPC], [0, 2], [BIN, E]], base=0, channel_multiplier=0,
                   allow_small_or_imprecise_dtypes=True).then_inc(s_const, 1)
            g.iota(slot_tile[:], pattern=[[1, SLOT_TILES], [0, E]], base=0, channel_multiplier=0,
                   allow_small_or_imprecise_dtypes=True).then_inc(s_const, 1)
            g.iota(rows1[:, :, C + A_TOK:C + A_TOK + 1].bitcast(I32), pattern=[[P, NT], [1, 1]], base=0,
                   channel_multiplier=1).then_inc(s_const, 1)
            g.memset(fill[:], 0.0).then_inc(s_fill, 1)
            pool.wait_ge(s_fill, 1)
            g.memset(fill[:, 2 * C + A_POS2:2 * C + A_TOK + 1].bitcast(I32), FILL).then_inc(s_fill, 1)

            rstd_out = (rs[:, 0, :], rs[:, 1, :], rows1[:, :, C + A_RSTD])

            def variance(n, t):
                return rows1[:, t, C + A_VAR] if n == 2 else mv[:, n, t, 1]

            def rstd(n, q):
                t = slice(q * TPC, (q + 1) * TPC)
                pool.wait_ge(s_mv[n], q + 1)
                g.tensor_scalar(veps[:, n, t], variance(n, t), LN_EPS, None, ALU.add).then_inc(s_ve[n], 1)
                pool.wait_ge(s_ve[n], q + 1)
                g.tensor_tensor(rstd_out[n][:, t], veps[:, n, t], minus_half[:, t], ALU.pow).then_inc(s_rs[n], 1)

            def clamp_k(q):
                c = q % 2
                pool.wait_ge(s_ke, q + 1)
                if q >= 2:
                    pool.wait_ge(s_sk, q - 1)
                    pool.wait_ge(s_uk, q - 1)
                g.tensor_scalar(ke[:, c], exp_k[:, c], EXP_MAX, None, ALU.min).then_inc(s_kc, 1)

            def wk_sum(q):
                b, c, o = q // QPB, q % 2, (q % QPB) * CHUNK
                pool.wait_ge(s_uk, q + 1)
                pool.wait_ge(s_sk, q + 1)
                if q >= 2:
                    pool.wait_ge(s_rec, q - 1)
                g.tensor_tensor(wks[:, c], uk[:, c], sum_k[:, b, o:o + CHUNK], ALU.add).then_inc(s_wks, 1)

            def rwkv(q):
                c = q % 2
                pool.wait_ge(s_wkv, q + 1)
                pool.wait_ge(s_rec, q + 1)
                g.tensor_tensor(yq[:, c], wkv[:, c], rec[:, c], ALU.mult).then_inc(s_yq, 1)

            def gated(q):
                c = q % 2
                pool.wait_ge(s_yq, q + 1)
                pool.wait_ge(s_sg, q + 1)
                if q >= 2:
                    pool.wait_ge(s_ops, q - 1)
                g.tensor_tensor(rw[:, c], sg[:, c], yq[:, c], ALU.mult).then_inc(s_rw, 1)

            def scatter1(q, part):
                i = q * TPC + part
                pool.wait_ge(s_pos, q + 1)
                pool.wait_ge(s_gates, q + 1)
                at = C + A_POS1
                g.indirect_dma_start(sorted1, bass.IndirectOffsetOnAxis(ap=rows1[:, i, at:at + 1].bitcast(I32), axis=0),
                                     rows1[:, i, :], None).then_inc(s_sc1, 16)

            pipeline(dict(rstd_x=lambda q: rstd(0, q), clamp_k=clamp_k, wk_sum=wk_sum, rwkv=rwkv, gated=gated,
                          rstd_o=lambda q: rstd(1, q), rstd_x1=lambda q: rstd(2, q),
                          scatter_0=lambda q: scatter1(q, 0), scatter_1=lambda q: scatter1(q, 1),
                          scatter_2=lambda q: scatter1(q, 2), scatter_3=lambda q: scatter1(q, 3)))
            for s in range(SLOT_TILES):
                pool.wait_ge(s_row, s + 1)
                at = 2 * C + A_POS2
                g.indirect_dma_start(sorted2, bass.IndirectOffsetOnAxis(ap=rows2[:, s, at:at + 1].bitcast(I32), axis=0),
                                     rows2[:, s, :], None, bounds_check=SLOTS - 1, oob_is_err=False).then_inc(s_sc2, 16)
            pool.wait_ge(s_out_x1, 16 * NQ)
            for s in range(SLOT_TILES):
                pool.wait_ge(s_yy, s + 1)
                at = 2 * C + A_TOK
                g.indirect_dma_start(out_rows, bass.IndirectOffsetOnAxis(ap=rows3[:, s, at:at + 1].bitcast(I32), axis=0),
                                     rows3[:, s, 0:C], None, bounds_check=TOKENS - 1, oob_is_err=False,
                                     compute_op=ALU.add).then_inc(s_out, 16)

        @block.scalar
        def _(act):
            a = nc.scalar
            act.preload_act_table(ACT.Exp)
            for n, w in ((0, wk), (2, wr)):
                act.dma_start(wnat[:, n, :], w).then_inc(s_wnat, 16)
            act.dma_start(mix[:], time_mix.rearrange("a b c -> c (a b)")).then_inc(s_small, 16)
            act.dma_start(decay_in[:], time_decay).then_inc(s_small, 16)
            act.dma_start(first_in[:], time_first).then_inc(s_small, 16)
            act.wait_ge(s_wtps, 1)
            a.activation(wT[:].rearrange("p n c -> p (n c)"), bank[2][:], ACT.Copy).then_inc(s_wt, 1)
            act.wait_ge(s_small, 16 * 3)
            a.activation(decay_e[:], decay_in[:], ACT.Exp).then_inc(s_par, 1)
            act.wait_ge(s_par, 1)
            a.activation(decay[:], decay_e[:], ACT.Exp, scale=-1.0).then_inc(s_par, 1)
            a.activation(first[:], first_in[:], ACT.Exp).then_inc(s_par, 1)
            act.wait_ge(s_par, 3)
            act.wait_ge(s_const, CONSTS)

            def norm_x(q):
                act.wait_ge(s_shx, q + 1)
                for i in range(q * TPC, (q + 1) * TPC):
                    ins = a.activation(xn[:, i, :], xin[:, i, :], ACT.Identity, bias=shift_in[:, i:i + 1],
                                       scale=rs[:, 0, i:i + 1])
                ins.then_inc(s_xn, 1)

            def xnt(q):
                b, c, o = q // QPB, q % 2, (q % QPB) * CHUNK
                act.wait_ge(s_xtps, q + 1)
                a.activation(xnT[:, b, 1 + o:1 + o + CHUNK], psX, ACT.Copy)
                if q >= 2:
                    act.wait_ge(s_xm, q - 1)
                a.activation(xmix[:, c], psX, ACT.Copy, scale=mix[:, 0:1]).then_inc(s_xt, 1)

            def kexp(q):
                c = q % 2
                act.wait_ge(s_kps, q + 1)
                if q >= 2:
                    act.wait_ge(s_kv, q - 1)
                    act.wait_ge(s_kc, q - 1)
                a.activation(exp_k[:, c], psK, ACT.Exp).then_inc(s_ke, 1)

            def sigmoid_uk(q):
                c = q % 2
                act.wait_ge(s_rps, q + 1)
                if q >= 2:
                    act.wait_ge(s_sg, q - 1)
                a.activation(th[:, c], psR, ACT.Tanh, scale=0.5).then_inc(s_th, 1)
                act.wait_ge(s_kc, q + 1)
                if q >= 2:
                    act.wait_ge(s_wks, q - 1)
                a.activation(uk[:, c], ke[:, c], ACT.Identity, bias=wk_eps[:, 0:1], scale=first[:, 0:1]).then_inc(s_uk, 1)
                act.wait_ge(s_th, q + 1)
                if q >= 2:
                    act.wait_ge(s_rw, q - 1)
                a.activation(sg[:, c], th[:, c], ACT.Identity, bias=all_ones[:, 0:1]).then_inc(s_sg, 1)

            def x1t(q):
                if q == 0:
                    act.wait_ge(s_b1ps, 1)
                    a.activation(w1_all[:, :, H:], bank[1][:, 0:E * HC].rearrange("p (e j) -> p e j", j=HC),
                                 ACT.Copy).then_inc(s_b1, 1)
                act.wait_ge(s_x1ps, q + 1)
                if q >= 2:
                    act.wait_ge(s_gps, q - 1)
                a.activation(x1T[:, q % 2], psX1, ACT.Copy).then_inc(s_x1t, 1)

            def gate_exp(q):
                t = slice(q * TPC, (q + 1) * TPC)
                act.wait_ge(s_dl, q + 1)
                a.activation(el[:, t], dl[:, t], ACT.Exp).then_inc(s_el, 1)

            pipeline(dict(norm_x=norm_x, copy_xn=xnt, exp_k=kexp, tanh_uk=sigmoid_uk, copy_x1=x1t, gate_exp=gate_exp))

            def xT_copy(n):
                act.wait_ge(s_tps, n + 1)
                if n >= 2:
                    act.wait_ge(s_hps, n - 1)
                a.activation(xT[:, n % 2], psT[n % 2][:, 0:P], ACT.Copy).then_inc(s_tsb, 1)

            def relu(n):
                act.wait_ge(s_hps, n + 1)
                if n >= 3:
                    act.wait_ge(s_eps, n - 2)
                for j in range(HC):
                    ins = a.activation(hT[:, n % 3, j * P:(j + 1) * P], psH[n % 2][:, j * P:(j + 1) * P],
                                       ACT.Relu, bias=w1s[:, n % STAGED, H + j:H + j + 1])
                ins.then_inc(s_h, 1)

            def deviation(n, s):
                t2 = pair(s)
                if t2:
                    act.wait_ge(s_mv2[n], s + 1)
                    a.activation(sd[:, n, t2], mv2[:, n, t2, 1], ACT.Sqrt, bias=ln_eps[:, 0:1]).then_inc(s_sd[n], 1)

            def outer(s):
                act.wait_ge(s_shift, pairs(s))
                a.activation(rows3[:, s, 0:C], rows3[:, s, C:2 * C], ACT.Identity, bias=shift[:, s:s + 1],
                             scale=rs2[:, 1, s:s + 1]).then_inc(s_yy, 1)

            act.preload_act_table(ACT.Sqrt)
            tile_pipeline([(1.11, xT_copy), (2.55, relu)])
            tile_pipeline([(1.54, lambda s: xT_copy(SLOT_TILES + s)), (2.89, lambda s: relu(SLOT_TILES + s)),
                           (5.82, lambda s: deviation(0, s)), (9.31, lambda s: deviation(1, s)), (10.93, outer)])

        @block.tensor
        def _(pe):
            t = nc.tensor
            pe.wait_ge(s_ident, 1)
            pe.wait_ge(s_wnat, 64)
            for n in range(4):
                ins = t.transpose(bank[2][:, n * C:(n + 1) * C], wnat[:, n, :], ident[:])
            ins.then_inc(s_wtps, 1)

            def transpose_params():
                pe.wait_ge(s_const, CONSTS)
                pe.wait_ge(s_gate, 32)
                t.matmul(bank[6][:, 0:E], all_ones[:], gw[:], start=True, stop=True).then_inc(s_gsum, 1)
                pe.wait_ge(s_moe, 16)
                t.transpose(bank[1][:, 0:E * HC], b1_rows[:], ident[0:E * HC, 0:E * HC]).then_inc(s_b1ps, 1)

            def transpose_xn(q):
                pe.wait_ge(s_xn, q + 1)
                if q >= 1:
                    pe.wait_ge(s_xt, q)
                for i in range(TPC):
                    ins = t.transpose(psX[:, i * P:(i + 1) * P], xn[:, q * TPC + i, :], ident[:])
                ins.then_inc(s_xtps, 1)

            def project_k(q):
                pe.wait_ge(s_xm, q + 1)
                if q == 0:
                    pe.wait_ge(s_wt, 1)
                else:
                    pe.wait_ge(s_ke, q)
                t.matmul(psK, wT[:, 0, :], xm[:, q % 3], start=True, stop=True).then_inc(s_kps, 1)

            def project_vr(q):
                if q >= 1:
                    pe.wait_ge(s_kv, q)
                t.matmul(psV, wT[:, 1, :], xm[:, q % 3], start=True, stop=True).then_inc(s_vps, 1)
                if q >= 1:
                    pe.wait_ge(s_th, q)
                t.matmul(psR, wT[:, 2, :], xm[:, q % 3], start=True, stop=True).then_inc(s_rps, 1)
                if q == 0:
                    transpose_params()

            def output(q):
                pe.wait_ge(s_rw, q + 1)
                if q >= 2:
                    pe.wait_ge(s_x1, q - 1)
                if q == 0:
                    pe.wait_ge(s_wo, 3)
                if q == 1:
                    pe.wait_ge(s_b1, 1)
                for i in range(TPC):
                    ins = t.matmul(psO[q % 2][:, i * P:(i + 1) * P], rw[:, q % 2, i * P:(i + 1) * P], wT[:, 3, :],
                                   start=True, stop=True)
                ins.then_inc(s_ops, 1)

            def transpose_x1(q):
                pe.wait_ge(s_x1, q + 1)
                if q >= 1:
                    pe.wait_ge(s_x1t, q)
                for i in range(TPC):
                    ins = t.transpose(psX1[:, i * P:(i + 1) * P], rows1[:, q * TPC + i, 0:C], ident[:])
                ins.then_inc(s_x1ps, 1)

            def gate(q):
                pe.wait_ge(s_x1t, q + 1)
                if q == 0:
                    pe.wait_ge(s_gwc, 1)
                if q >= 1:
                    pe.wait_ge(s_placed, q)
                for i in range(TPC):
                    n = q * TPC + i
                    ins = t.matmul(psG[:, n * E:(n + 1) * E], x1T[:, q % 2, i * P:(i + 1) * P], gwc[:],
                                   start=True, stop=True)
                ins.then_inc(s_gps, 1)

            def places(q):
                at = psP[:, q * TPC * 2 * E:(q + 1) * TPC * 2 * E].rearrange("p (n r e) -> p n (r e)", n=TPC, e=E)
                hots = hot[:].rearrange("p n r e -> p n (r e)")
                pe.wait_ge(s_sc, q + 1)
                t.matmul(at, ones_row[0:1, :], bin_start[:].rearrange("p n r e -> p n (r e)"), start=True, stop=False)
                for j in range(q * TPC):
                    t.matmul(at, ones_b[:], hots[:, j:j + 1].to_broadcast([P, TPC, 2 * E]), start=False, stop=False)
                pe.wait_ge(s_hot, q + 1)
                for j in range(TPC - 1):
                    t.matmul(at[:, j + 1:], ones_b[:], hots[:, q * TPC + j, None].to_broadcast([P, TPC - 1 - j, 2 * E]),
                             start=False, stop=False)
                t.matmul(at, before[:], hots[:, q * TPC:(q + 1) * TPC], start=False, stop=True).then_inc(s_cnt, 1)
                if q == NQ - 1:
                    pe.wait_ge(s_ke, NQ)
                    for j in range(NT):
                        ins = t.matmul(psN, ones_b[:], hots[:, j], start=(j == 0), stop=(j == NT - 1))
                    ins.then_inc(s_bins, 1)

            pipeline(dict(transpose_xn=transpose_xn, project_k=project_k, project_vr=project_vr, output=output,
                          transpose_x1=transpose_x1, gate=gate, places=places))

            def expert_of(r):
                return nc.values_load_multi_w_load_instructions(
                    eid[0:1, r, :], engines=[mybir.EngineType.PE], min_val=0, max_val=E - 1,
                    skip_runtime_bounds_check_because="a count from 0, cut off at E - 1")[1]

            def turn(n):
                s = n % SLOT_TILES
                if n < SLOT_TILES:
                    pe.wait_ge(s_xs, n + 1)
                    src = rows2[:, s, C:2 * C]
                else:
                    pe.wait_ge(s_in3[s % LOADS], 16 * (s // LOADS + 1))
                    src = rows3[:, s, 0:C]
                if n >= 2:
                    pe.wait_ge(s_tsb, n - 1)
                t.transpose(psT[n % 2][:, 0:P], src, ident[:]).then_inc(s_tps, 1)

            def hidden(n):
                pe.wait_ge(s_tsb, n + 1)
                if n < SLOT_TILES:
                    pe.wait_ge(s_w1d, n + 1)
                else:
                    before_n = len([m for m in range(SLOT_TILES, n) if m % STAGED == n % STAGED])
                    pe.wait_ge(s_w1s[n % STAGED], 16 * (before_n + 1))
                if n >= 2:
                    pe.wait_ge(s_h, n - 1)
                for j in range(HC):
                    ins = t.matmul(psH[n % 2][:, j * P:(j + 1) * P], w1s[:, n % STAGED, j * P:(j + 1) * P],
                                   xT[:, n % 2], start=True, stop=True)
                ins.then_inc(s_hps, 1)

            w2f = w2_all[:].rearrange("p a d -> p (a d)")

            def second(n, e):
                pe.wait_ge(s_h, n + 1)
                if 2 <= n < SLOT_TILES + 2:
                    pe.wait_ge(s_row, n - 1)
                elif n >= 2:
                    pe.wait_ge(s_res, n - 1 - SLOT_TILES)
                for j in range(HC):
                    t.matmul(psE[n % 2][:, 0:C], hT[:, n % 3, j * P:(j + 1) * P],
                             w2f[:, bass.ds(e * (HC * C) + j * C, C)], start=(j == 0), stop=False)
                t.matmul(psE[n % 2][:, 0:C], ones_row[:], b2_split[:, bass.ds(e * C, C)],
                         start=False, stop=True).then_inc(s_eps, 1)

            def keep_clock_up(n):
                for _ in range(n):
                    t.matmul(bank[4][:], ones_b[:], spin[:], start=True, stop=True)

            pe.wait_ge(s_th, NQ)
            pe.wait_ge(s_eid, 1)
            keep_clock_up(16)
            pe.wait_ge(s_w2, 16)
            pe.wait_ge(s_b2r, 48)
            first_expert = expert_of(0)
            tile_pipeline([(0.55, turn), (1.86, hidden), (3.47, lambda s: second(s, first_expert[s]))])
            keep_clock_up(28)
            pe.wait_ge(s_eid, 2)
            second_expert = expert_of(1)
            tile_pipeline([(0.72, lambda s: turn(SLOT_TILES + s)), (2.29, lambda s: hidden(SLOT_TILES + s)),
                           (3.7, lambda s: second(SLOT_TILES + s, second_expert[s]))])

        @block.vector
        def _(dve):
            v = nc.vector
            moments_out = [(lambda i, n=n: mv[:, n, i, :]) for n in range(2)]
            moments_out.append(lambda i: rows1[:, i, C + A_MEAN:C + A_VAR + 1])

            def moments(n, q, src):
                for i in range(TPC):
                    v_ = v.bn_stats(st[:, n, q * TPC + i, :], src(i))
                v_.then_inc(s_st[n], 1)
                dve.wait_ge(s_st[n], q + 1)
                for i in range(TPC):
                    v_ = v.bn_aggr(moments_out[n](q * TPC + i), st[:, n, q * TPC + i, :])
                v_.then_inc(s_mv[n], 1)

            def stats_x(q):
                dve.wait_ge(s_x[q], 16)
                moments(0, q, lambda i: xin[:, q * TPC + i, :])

            def shift_x(q):
                t = tiles_of(q)
                dve.wait_ge(s_rs[0], q + 1)
                v.scalar_tensor_tensor(shift_in[:, t], mv[:, 0, t, 0], -1.0, rs[:, 0, t], ALU.mult,
                                       ALU.mult).then_inc(s_shx, 1)

            def center_wo():
                dve.wait_ge(s_wt, 1)
                v.tensor_reduce(wo_sum[:], wT[:, 3, :], AXX, ALU.add).then_inc(s_wo, 1)
                dve.wait_ge(s_wo, 1)
                v.tensor_scalar(wo_mean[:], wo_sum[:], 1.0 / C, None, ALU.mult).then_inc(s_wo, 1)
                dve.wait_ge(s_wo, 2)
                v.tensor_scalar(wT[:, 3, :], wT[:, 3, :], wo_mean[:, 0:1], 0.5, ALU.subtract, ALU.mult).then_inc(s_wo, 1)

            def center_gate():
                dve.wait_ge(s_gsum, 1)
                v.scalar_tensor_tensor(gwc[:], bank[6][:, 0:E], -1.0 / C, gw[:], ALU.mult, ALU.add).then_inc(s_gwc, 1)

            def split_b2():
                dve.wait_ge(s_b2, 16)
                v.tensor_copy(b2_part[:, 0, :], b2_rows[:]).then_inc(s_b2s, 1)
                dve.wait_ge(s_b2s, 1)
                v.tensor_tensor(b2_rows[:], b2_rows[:], b2_part[:, 0, :], ALU.subtract).then_inc(s_b2s, 1)
                dve.wait_ge(s_b2s, 2)
                v.tensor_copy(b2_part[:, 1, :], b2_rows[:]).then_inc(s_b2s, 1)
                dve.wait_ge(s_b2s, 3)
                v.tensor_tensor(b2_rows[:], b2_rows[:], b2_part[:, 1, :], ALU.subtract).then_inc(s_b2s, 1)
                dve.wait_ge(s_b2s, 4)
                v.tensor_copy(b2_part[:, 2, :], b2_rows[:]).then_inc(s_b2s, 1)

            def mix_x(q):
                b, c, o = q // QPB, q % 2, (q % QPB) * CHUNK
                dve.wait_ge(s_xt, q + 1)
                if q == 0:
                    dve.wait_ge(s_small, 16 * 3)
                    v.tensor_scalar(mix_rest[:], mix[:], -1.0, 1.0, ALU.mult, ALU.add).then_inc(s_rest, 1)
                    dve.wait_ge(s_rest, 1)
                    dve.wait_ge(s_par, 3)
                    dve.wait_ge(s_const, CONSTS)
                if q >= 3:
                    dve.wait_ge(s_rps, q - 2)
                v.scalar_tensor_tensor(xm[:, q % 3], xnT[:, b, o:o + CHUNK], mix_rest[:, 0:1], xmix[:, c],
                                       ALU.mult, ALU.add).then_inc(s_xm, 1)
                if q == 0:
                    center_wo()
                    split_b2()

            def scans(q):
                b, c, o = q // QPB, q % 2, (q % QPB) * CHUNK
                dve.wait_ge(s_ke, q + 1)
                dve.wait_ge(s_vps, q + 1)
                v.scalar_tensor_tensor(kv[:, c], exp_k[:, c], EXP_MAX, psV, ALU.min, ALU.mult).then_inc(s_kv, 1)
                lam = decay[:, 0:1].to_broadcast([P, CHUNK])
                if q >= 1:
                    dve.wait_ge(s_skv, q)
                dve.wait_ge(s_kc, q + 1)
                v.tensor_tensor_scan(sum_k[:, b, 1 + o:1 + o + CHUNK], lam, ke[:, c],
                                     sum_k[:, b, o:o + 1], ALU.mult, ALU.add).then_inc(s_sk, 1)
                dve.wait_ge(s_kv, q + 1)
                v.tensor_tensor_scan(sum_kv[:, b, 1 + o:1 + o + CHUNK], lam, kv[:, c],
                                     sum_kv[:, b, o:o + 1], ALU.mult, ALU.add).then_inc(s_skv, 1)

            def quotient(q):
                b, c, o = q // QPB, q % 2, (q % QPB) * CHUNK
                dve.wait_ge(s_skv, q + 1)
                if q >= 2:
                    dve.wait_ge(s_yq, q - 1)
                v.scalar_tensor_tensor(wkv[:, c], kv[:, c], first[:, 0:1], sum_kv[:, b, o:o + CHUNK],
                                       ALU.mult, ALU.add).then_inc(s_wkv, 1)
                dve.wait_ge(s_wks, q + 1)
                v.reciprocal(rec[:, c], wks[:, c]).then_inc(s_rec, 1)

            def stats_o(q):
                if q == 0:
                    center_gate()
                dve.wait_ge(s_ops, q + 1)
                moments(1, q, lambda i: psO[q % 2][:, i * P:(i + 1) * P])

            def residual(q):
                dve.wait_ge(s_rs[1], q + 1)
                for i in range(TPC):
                    n = q * TPC + i
                    v_ = v.scalar_tensor_tensor(rows1[:, n, 0:C], psO[q % 2][:, i * P:(i + 1) * P], rs[:, 1, n:n + 1],
                                                xin[:, n, :], ALU.mult, ALU.add)
                v_.then_inc(s_x1, 1)

            def stats_x1(q):
                dve.wait_ge(s_x1, q + 1)
                moments(2, q, lambda i: rows1[:, q * TPC + i, 0:C])

            def scale_logits(q):
                dve.wait_ge(s_gps, q + 1)
                dve.wait_ge(s_rs[2], q + 1)
                tt = tiles_of(q)
                v.tensor_tensor(scaled[:, tt], psG.rearrange("p (n e) -> p n e", e=E)[:, tt],
                                rows1[:, tt, C + A_RSTD:C + A_RSTD + 1].to_broadcast([P, TPC, E]), ALU.mult).then_inc(s_sc, 1)

            def add_gate_bias(q):
                dve.wait_ge(s_sc, q + 1)
                dve.wait_ge(s_gate, 32)
                tt = tiles_of(q)
                v.tensor_tensor(logit[:, tt], scaled[:, tt], gb[:, None, :].to_broadcast([P, TPC, E]),
                                ALU.add).then_inc(s_lo, 1)

            def sort_logits(q):
                dve.wait_ge(s_lo, q + 1)
                for i in range(q * TPC, (q + 1) * TPC):
                    v_ = v.max(top[:, i, :], logit[:, i, :])
                v_.then_inc(s_top, 1)

            def sort_experts(q):
                dve.wait_ge(s_top, q + 1)
                for i in range(q * TPC, (q + 1) * TPC):
                    v_ = v.max_index(topi[:, i, :], top[:, i, :], logit[:, i, :])
                v_.then_inc(s_topi, 1)

            def onehots(q):
                dve.wait_ge(s_topi, q + 1)
                tt = tiles_of(q)
                v.tensor_tensor(hot[:, tt], expert_no[:, None, None, :].to_broadcast([P, TPC, 2, E]),
                                topi[:, tt, 0:2, None].to_broadcast([P, TPC, 2, E]), ALU.is_equal).then_inc(s_hot, 1)

            def gate_shift(q):
                tt = tiles_of(q)
                v.tensor_tensor(dl[:, tt], top[:, tt], top[:, tt, 0:1].to_broadcast([P, TPC, E]),
                                ALU.subtract).then_inc(s_dl, 1)

            def gates(q):
                tt = tiles_of(q)
                dve.wait_ge(s_el, q + 1)
                v.tensor_reduce(den[:, tt], el[:, tt], AXX, ALU.add).then_inc(s_den, 1)
                dve.wait_ge(s_den, q + 1)
                v.reciprocal(rows1[:, tt, C + A_G0], den[:, tt]).then_inc(s_g0, 1)
                dve.wait_ge(s_g0, q + 1)
                v.tensor_tensor(rows1[:, tt, C + A_G1], el[:, tt, 1], rows1[:, tt, C + A_G0], ALU.mult).then_inc(s_gates, 1)

            def place(q):
                tt = tiles_of(q)
                dve.wait_ge(s_cnt, q + 1)
                v.tensor_tensor(placed[:, tt], psP[:, q * TPC * 2 * E:(q + 1) * TPC * 2 * E].rearrange("p (n r e) -> p n r e", r=2, e=E),
                                hot[:, tt], ALU.mult).then_inc(s_placed, 1)
                dve.wait_ge(s_placed, q + 1)
                with nc.allow_low_precision(reason="slots are whole numbers far below 2 ** 24"):
                    v.tensor_reduce(rows1[:, tt, C + A_POS1:C + A_POS2 + 1].bitcast(I32), placed[:, tt], AXX,
                                    ALU.add).then_inc(s_pos, 1)

            pipeline(dict(stats_x=stats_x, shift_x=shift_x, mix_x=mix_x, kv_scans=scans,
                          quotient=quotient, stats_o=stats_o, residual=residual, stats_x1=stats_x1,
                          scale_logits=scale_logits, add_gate_bias=add_gate_bias, sort_logits=sort_logits,
                          sort_experts=sort_experts, gate_shift=gate_shift, onehots=onehots, gates=gates,
                          place=place))

            count = [0]

            def step(ins):
                ins.then_inc(s_tr, 1)
                count[0] += 1
                dve.wait_ge(s_tr, count[0])

            dve.wait_ge(s_bins, 1)
            counts = psN[0:1, :].rearrange("p (r e) -> p r e", e=E)
            v.tensor_copy(count_i[:], counts).then_inc(s_cn, 1)
            step(v.tensor_scalar(count_up[:], counts, float(P - 1), None, ALU.add))
            step(v.tensor_scalar(ntile_i[:], count_up[:], P.bit_length() - 1, None, ALU.logical_shift_right))
            step(v.tensor_scalar(skip[:], ntile_i[:], -1.0, float(BIN_TILES), ALU.mult, ALU.add))
            for r in range(2):
                step(v.tensor_tensor_scan(cum[:, r], keep_e[:], ntile_i[:, r], 0.0, ALU.mult, ALU.add))
                step(v.tensor_tensor(done_e[:, r], cum[:, r, None, :].to_broadcast([1, SLOT_TILES, E]), slot_tile[:],
                                     ALU.is_le))
                step(v.tensor_reduce(eid_f[:, r], done_e[:, r], AXX, ALU.add))
                v.tensor_scalar(eid[:, r], eid_f[:, r], float(E - 1), None, ALU.min)
                step(v.tensor_tensor(skipped[:, r], done_e[:, r], skip[:, r, None, :].to_broadcast([1, SLOT_TILES, E]),
                                     ALU.mult))
                step(v.tensor_reduce(tid_f[:, r], skipped[:, r], AXX, ALU.add))
                step(v.tensor_tensor(tid_s[:, r], tid_f[:, r], slot_tile[:, :, 0], ALU.add))
                v.tensor_scalar(tid[:, r], tid_s[:, r], float(NO_TILE), None, ALU.min).then_inc(s_eid, 1)
            dve.wait_ge(s_eid, 1)

            def aux(rows, s, what):
                return rows[:, s, 2 * C + what:2 * C + what + 1]

            def norm_rows(s):
                dve.wait_ge(s_in2[s % LOADS], 16 * (s // LOADS + 1))
                v.tensor_scalar(rows2[:, s, C:2 * C], rows2[:, s, C:2 * C], aux(rows2, s, A_MEAN),
                                aux(rows2, s, A_RSTD), ALU.subtract, ALU.mult).then_inc(s_xs, 1)

            def write_row(s):
                dve.wait_ge(s_eps, s + 1)
                v.scalar_tensor_tensor(rows2[:, s, 0:C], psE[s % 2][:, 0:C], ALPHA, rows2[:, s, C:2 * C],
                                       ALU.mult, ALU.add)
                v.scalar_tensor_tensor(rows2[:, s, C:2 * C], psE[s % 2][:, 0:C], aux(rows2, s, A_G0),
                                       rows2[:, s, C:2 * C], ALU.mult, ALU.add).then_inc(s_row, 1)

            w1f = w1_all[:].rearrange("p e h -> p (e h)")

            def stage_w1(s, e):
                if s >= STAGED:
                    dve.wait_ge(s_h, s - STAGED + 1)
                v.tensor_copy(w1s[:, s % STAGED, :], w1f[:, bass.ds(e * (H + HC), H + HC)]).then_inc(s_w1d, 1)

            dve.wait_ge(s_w1, 16)
            dve.wait_ge(s_b1, 1)
            first_expert = nc.values_load_multi_w_load_instructions(
                eid[0:1, 0, :], engines=[mybir.EngineType.DVE], min_val=0, max_val=E - 1,
                skip_runtime_bounds_check_because="a count from 0, cut off at E - 1")[1]
            tile_pipeline([(-0.72, lambda s: stage_w1(s, first_expert[s])), (-0.74, norm_rows), (4.33, write_row)])

            low, mid = (lambda s: rows3[:, s, 0:C]), (lambda s: rows3[:, s, C:2 * C])

            def add_choice(s):
                n = SLOT_TILES + s
                dve.wait_ge(s_eps, n + 1)
                dve.wait_ge(s_in3[s % LOADS], 16 * (s // LOADS + 1))
                v.scalar_tensor_tensor(mid(s), psE[n % 2][:, 0:C], aux(rows3, s, A_G1), mid(s),
                                       ALU.mult, ALU.add).then_inc(s_res, 1)

            def stats2(n, s):
                dve.wait_ge((s_res, s_zz)[n], s + 1)
                v.bn_stats(st2[:, n, s, :], mid(s)).then_inc(s_st2[n], 1)

            def moments2(n, s):
                dve.wait_ge(s_st2[n], s + 1)
                v.bn_aggr(mv2[:, n, s, :], st2[:, n, s, :]).then_inc(s_mv2[n], 1)

            def times_gamma(s):
                dve.wait_ge(s_mv2[0], s + 1)
                dve.wait_ge(s_tps, SLOT_TILES + s + 1)
                v.scalar_tensor_tensor(low(s), mid(s), mv2[:, 0, s, 0:1], gamma[:], ALU.subtract,
                                       ALU.mult).then_inc(s_tg, 1)

            def rstd2(n, s):
                t2 = pair(s)
                if t2:
                    dve.wait_ge(s_sd[n], pairs(s))
                    v.reciprocal(rs2[:, n, t2], sd[:, n, t2]).then_inc(s_rs2[n], 1)

            def inner(s):
                dve.wait_ge(s_tg, s + 1)
                dve.wait_ge(s_rs2[0], pairs(s))
                v.scalar_tensor_tensor(mid(s), low(s), rs2[:, 0, s:s + 1], beta[:], ALU.mult,
                                       ALU.add).then_inc(s_zz, 1)

            def outer_shift(s):
                t2 = pair(s)
                if t2:
                    dve.wait_ge(s_rs2[1], pairs(s))
                    v.scalar_tensor_tensor(shift[:, t2], mv2[:, 1, t2, 0], -1.0, rs2[:, 1, t2],
                                           ALU.mult, ALU.mult).then_inc(s_shift, 1)

            dve.wait_ge(s_norm, 32)
            tile_pipeline([(5.03, add_choice), (5.22, lambda s: stats2(0, s)), (5.64, lambda s: moments2(0, s)),
                           (6.08, times_gamma), (6.75, lambda s: rstd2(0, s)), (8.14, inner),
                           (8.37, lambda s: stats2(1, s)), (9.05, lambda s: moments2(1, s)),
                           (10.0, lambda s: rstd2(1, s)), (10.07, outer_shift)])


_INS = ['L0_attn_x', 'L0_attn_time_decay', 'L0_attn_time_first', 'L0_attn_time_mix', 'L0_attn_Wk',
        'L0_attn_Wv', 'L0_attn_Wr', 'L0_attn_Wo', 'L0_ffn_gate_W', 'L0_ffn_gate_b', 'L0_ffn_W1',
        'L0_ffn_b1', 'L0_ffn_W2', 'L0_ffn_b2', 'L0_ffn_ln_gamma', 'L0_ffn_ln_beta']


def kernel(**inputs):
    import numpy as np
    import concourse.bacc as bacc
    from concourse.bass_utils import run_bass_kernel_spmd as run

    nc = bacc.Bacc("TRN2", target_bir_lowering=False, num_devices=1)
    arrays, args = {}, []
    for name in _INS:
        a = np.ascontiguousarray(inputs[name])
        arrays[f"in_{name}"] = a
        args.append(nc.dram_tensor(f"in_{name}", a.shape, mybir.dt.from_np(a.dtype), kind="ExternalInput").ap())
    o = nc.dram_tensor("o", arrays["in_L0_attn_x"].shape, F32, kind="ExternalOutput").ap()
    build_program(nc, *args, o)
    r = run(nc, [arrays], core_ids=[0])
    return r.results[0]["o"]
```
